# Optimizing a Trainium2 kernel written in Bass

```python
import numpy as np
import jax
import jax.numpy as jnp

def _softmax(x, axis=-1):
    return jax.nn.softmax(x, axis=axis)

def _gelu(x):
    return jax.nn.gelu(x, approximate=True)

def _silu(x):
    return jax.nn.silu(x)

def _sigmoid(x):
    return jax.nn.sigmoid(x)

def _layernorm(x, axis=-1, eps=1e-05):
    m = jnp.mean(x, axis=axis, keepdims=True)
    v = jnp.var(x, axis=axis, keepdims=True)
    return (x - m) / jnp.sqrt(v + eps)

def _scatter_add(tgt, idx, src, axis=0):
    return tgt.at[idx].add(src)

def _segment_sum(src, seg, n):
    return jax.ops.segment_sum(src, seg, n)
kernel_name = 'mk_gnn_resnorm_d2_gnn_r8_756aa2'

def setup_inputs(seed: int=0):
    np.random.seed(seed)
    _w = jnp.asarray

    def _rec_inputs():
        import jax
        import jax.numpy as jnp
        _gk = jax.random.key(seed)
        x = -0.0001126 + 1 * jax.random.normal(jax.random.fold_in(_gk, 1), (12500, 256), jnp.float32)
        _s = jax.random.randint(jax.random.fold_in(_gk, 2), (100000,), 0, 12500, jnp.int32)
        _d = jax.random.randint(jax.random.fold_in(_gk, 3), (100000,), 0, 12500, jnp.int32)
        _loop = jnp.arange(12500, dtype=jnp.int32)
        src = jnp.concatenate([_s, _d, _loop])
        dst = jnp.concatenate([_d, _s, _loop])
        _o = jnp.argsort(dst, stable=True)
        src = src[_o]
        dst = dst[_o]
        edge_attr_4 = 0.00117183 + 1.0004 * jax.random.normal(jax.random.fold_in(_gk, 12), (212500, 4), jnp.float32)
        edge_attr_8 = -0.000615933 + 0.999959 * jax.random.normal(jax.random.fold_in(_gk, 13), (212500, 8), jnp.float32)
        node_vec1 = jax.random.uniform(jax.random.fold_in(_gk, 15), (12500, 1), jnp.float32, 0.0, 1)
        return (x, src, dst, edge_attr_4, edge_attr_8, node_vec1)
    x, src, dst, edge_attr_4, edge_attr_8, node_vec1 = _rec_inputs()

    def _L0_gnn_setup():
        import jax, jax.numpy as jnp
        import numpy as np
        import math
        N = 3750
        E = 75000
        MUL = 64
        NES = 8
        FCN = 64
        NUM_NEIGHBORS = 20.0
        SILU_NORM = 1.679
        INV_SQRT3 = 1.0 / math.sqrt(3.0)

        def _split(x):
            return (x[:, :MUL], x[:, MUL:].reshape(-1, MUL, 3))
        key = jax.random.key(seed)
        ks = jax.random.split(key, 16)
        inp = {'node_input': jax.random.normal(ks[0], (N, 4 * MUL), jnp.float32), 'node_attr': jnp.ones((N, 1), jnp.float32), 'edge_src': jax.random.randint(ks[1], (E,), 0, N), 'edge_dst': jax.random.randint(ks[2], (E,), 0, N), 'edge_attr': jax.random.normal(ks[3], (E, 4), jnp.float32), 'edge_scalars': jax.random.normal(ks[4], (E, NES), jnp.float32), 'sc_w0': jax.random.normal(ks[5], (MUL, MUL), jnp.float32), 'sc_w1': jax.random.normal(ks[6], (MUL, MUL), jnp.float32), 'lin1_w0': jax.random.normal(ks[7], (MUL, MUL), jnp.float32), 'lin1_w1': jax.random.normal(ks[8], (MUL, MUL), jnp.float32), 'fc_w1': jax.random.normal(ks[9], (NES, FCN), jnp.float32), 'fc_w2': jax.random.normal(ks[10], (FCN, 4 * MUL), jnp.float32), 'lin2_w00': jax.random.normal(ks[11], (MUL, MUL), jnp.float32), 'lin2_w01': jax.random.normal(ks[12], (MUL, MUL), jnp.float32), 'lin2_w10': jax.random.normal(ks[13], (MUL, MUL), jnp.float32), 'lin2_w11': jax.random.normal(ks[14], (MUL, MUL), jnp.float32)}
        return inp
    _L0_gnn_all = _L0_gnn_setup()
    _L0_gnn_in = {k: v for k, v in _L0_gnn_all.items() if k in ('sc_w0', 'sc_w1', 'lin1_w0', 'lin1_w1', 'fc_w1', 'fc_w2', 'lin2_w00', 'lin2_w01', 'lin2_w10', 'lin2_w11')}
    del _L0_gnn_all

    def _L1_gnn_setup():
        import jax, jax.numpy as jnp
        import numpy as np
        N_NODES = 6250
        N_EDGES = 100000
        IN_CH = 256
        HEADS = 8
        HEAD_DIM = 32
        NEG_SLOPE = 0.2
        LN_EPS = 1e-05
        SOFTMAX_EPS = 1e-16
        key = jax.random.key(seed)
        k1, k2, k3, k4 = jax.random.split(key, 4)
        x = jax.random.normal(k1, (N_NODES, IN_CH), dtype=jnp.float32)
        edge_index = jax.random.randint(k2, (2, N_EDGES), 0, N_NODES, dtype=jnp.int64)
        lin_w = jax.random.normal(k3, (IN_CH, HEADS * HEAD_DIM), dtype=jnp.float32) * (1.0 / np.sqrt(IN_CH))
        att = jax.random.normal(k4, (HEADS, 2 * HEAD_DIM), dtype=jnp.float32) * 0.1
        ln_w = jnp.ones((HEADS * HEAD_DIM,), dtype=jnp.float32)
        ln_b = jnp.zeros((HEADS * HEAD_DIM,), dtype=jnp.float32)
        return {'x': x, 'edge_index': edge_index, 'lin_w': lin_w, 'att': att, 'ln_w': ln_w, 'ln_b': ln_b}
    _L1_gnn_all = _L1_gnn_setup()
    _L1_gnn_in = {k: v for k, v in _L1_gnn_all.items() if k in ('lin_w', 'att', 'ln_w', 'ln_b')}
    del _L1_gnn_all
    return {'x': x, 'src': src, 'dst': dst, 'edge_attr_4': edge_attr_4, 'edge_attr_8': edge_attr_8, 'node_vec1': node_vec1, 'L0_gnn_sc_w0': _L0_gnn_in['sc_w0'], 'L0_gnn_sc_w1': _L0_gnn_in['sc_w1'], 'L0_gnn_lin1_w0': _L0_gnn_in['lin1_w0'], 'L0_gnn_lin1_w1': _L0_gnn_in['lin1_w1'], 'L0_gnn_fc_w1': _L0_gnn_in['fc_w1'], 'L0_gnn_fc_w2': _L0_gnn_in['fc_w2'], 'L0_gnn_lin2_w00': _L0_gnn_in['lin2_w00'], 'L0_gnn_lin2_w01': _L0_gnn_in['lin2_w01'], 'L0_gnn_lin2_w10': _L0_gnn_in['lin2_w10'], 'L0_gnn_lin2_w11': _L0_gnn_in['lin2_w11'], 'L1_gnn_lin_w': _L1_gnn_in['lin_w'], 'L1_gnn_att': _L1_gnn_in['att'], 'L1_gnn_ln_w': _L1_gnn_in['ln_w'], 'L1_gnn_ln_b': _L1_gnn_in['ln_b']}

def reference(x, src, dst, edge_attr_4, edge_attr_8, node_vec1, L0_gnn_sc_w0, L0_gnn_sc_w1, L0_gnn_lin1_w0, L0_gnn_lin1_w1, L0_gnn_fc_w1, L0_gnn_fc_w2, L0_gnn_lin2_w00, L0_gnn_lin2_w01, L0_gnn_lin2_w10, L0_gnn_lin2_w11, L1_gnn_lin_w, L1_gnn_att, L1_gnn_ln_w, L1_gnn_ln_b):
    import jax
    import jax.numpy as jnp

    def _L0_gnn_ref(node_input, node_attr, edge_src, edge_dst, edge_attr, edge_scalars, sc_w0, sc_w1, lin1_w0, lin1_w1, fc_w1, fc_w2, lin2_w00, lin2_w01, lin2_w10, lin2_w11):
        import jax, jax.numpy as jnp
        import numpy as np
        import math
        N = 3750
        E = 75000
        MUL = 64
        NES = 8
        FCN = 64
        NUM_NEIGHBORS = 20.0
        SILU_NORM = 1.679
        INV_SQRT3 = 1.0 / math.sqrt(3.0)

        def _split(x):
            return (x[:, :MUL], x[:, MUL:].reshape(-1, MUL, 3))
        n = node_input.shape[0]
        inv_mul = 1.0 / math.sqrt(MUL)
        x0, x1 = _split(node_input)
        a = node_attr
        s0 = x0 @ sc_w0 * a * inv_mul
        s1 = jnp.einsum('nuc,uv->nvc', x1, sc_w1) * a[:, :, None] * inv_mul
        y0 = x0 @ lin1_w0 * a * inv_mul
        y1 = jnp.einsum('nuc,uv->nvc', x1, lin1_w1) * a[:, :, None] * inv_mul
        h = jax.nn.silu(edge_scalars @ fc_w1 * (1.0 / math.sqrt(NES))) * SILU_NORM
        w = h @ fc_w2 * (1.0 / math.sqrt(FCN))
        w_a, w_b, w_c, w_d = (w[:, :MUL], w[:, MUL:2 * MUL], w[:, 2 * MUL:3 * MUL], w[:, 3 * MUL:])
        xg0 = y0[edge_src]
        xg1 = y1[edge_src]
        ea0 = edge_attr[:, :1]
        ea1 = edge_attr[:, 1:4]
        mid0 = w_a * xg0 * ea0
        mid1 = w_b * jnp.einsum('euc,ec->eu', xg1, ea1) * INV_SQRT3
        mid2 = (w_c * xg0)[:, :, None] * ea1[:, None, :]
        mid3 = (w_d * ea0)[:, :, None] * xg1
        mids = jnp.concatenate([mid0, mid1, mid2.reshape(-1, 3 * MUL), mid3.reshape(-1, 3 * MUL)], axis=1)
        agg = jax.ops.segment_sum(mids, edge_dst, num_segments=n)
        agg = agg * (1.0 / math.sqrt(NUM_NEIGHBORS))
        z0a = agg[:, :MUL]
        z0b = agg[:, MUL:2 * MUL]
        z1a = agg[:, 2 * MUL:5 * MUL].reshape(n, MUL, 3)
        z1b = agg[:, 5 * MUL:].reshape(n, MUL, 3)
        inv2 = 1.0 / math.sqrt(2 * MUL)
        o0 = (z0a @ lin2_w00 + z0b @ lin2_w01) * a * inv2
        o1 = (jnp.einsum('nuc,uv->nvc', z1a, lin2_w10) + jnp.einsum('nuc,uv->nvc', z1b, lin2_w11)) * a[:, :, None] * inv2
        c_s = math.sin(math.pi / 8.0)
        c_x = math.cos(math.pi / 8.0)
        out0 = c_s * s0 + c_x * o0
        out1 = c_s * s1 + c_x * o1
        return jnp.concatenate([out0, out1.reshape(n, 3 * MUL)], axis=1)

    def _L1_gnn_ref(x, edge_index, lin_w, att, ln_w, ln_b):
        import jax, jax.numpy as jnp
        import numpy as np
        N_NODES = 6250
        N_EDGES = 100000
        IN_CH = 256
        HEADS = 8
        HEAD_DIM = 32
        NEG_SLOPE = 0.2
        LN_EPS = 1e-05
        SOFTMAX_EPS = 1e-16
        N = x.shape[0]
        src, dst = (edge_index[0], edge_index[1])
        xp = (x @ lin_w).reshape(N, HEADS, HEAD_DIM)
        att_i, att_j = (att[:, :HEAD_DIM], att[:, HEAD_DIM:])
        a_i = jnp.einsum('nhc,hc->nh', xp, att_i)
        a_j = jnp.einsum('nhc,hc->nh', xp, att_j)
        alpha = a_i[dst] + a_j[src]
        alpha = jnp.where(alpha >= 0, alpha, NEG_SLOPE * alpha)
        amax = jax.ops.segment_max(alpha, dst, num_segments=N)
        amax = jnp.where(jnp.isfinite(amax), amax, 0.0)
        ex = jnp.exp(alpha - amax[dst])
        denom = jax.ops.segment_sum(ex, dst, num_segments=N)
        alpha = ex / (denom[dst] + SOFTMAX_EPS)
        msg = xp[src] * alpha[:, :, None]
        out = jax.ops.segment_sum(msg, dst, num_segments=N)
        out = out.reshape(N, HEADS * HEAD_DIM)
        mu = out.mean(axis=-1, keepdims=True)
        var = ((out - mu) ** 2).mean(axis=-1, keepdims=True)
        out = (out - mu) * jax.lax.rsqrt(var + LN_EPS) * ln_w + ln_b
        out = jax.nn.elu(out)
        return out + x
    edge_index = jnp.stack([src, dst])
    x = _layernorm(x + _L0_gnn_ref(x, node_vec1, src, dst, edge_attr_4, edge_attr_8, L0_gnn_sc_w0, L0_gnn_sc_w1, L0_gnn_lin1_w0, L0_gnn_lin1_w1, L0_gnn_fc_w1, L0_gnn_fc_w2, L0_gnn_lin2_w00, L0_gnn_lin2_w01, L0_gnn_lin2_w10, L0_gnn_lin2_w11), axis=-1)
    x = _layernorm(x + _L1_gnn_ref(x, edge_index, L1_gnn_lin_w, L1_gnn_att, L1_gnn_ln_w, L1_gnn_ln_b), axis=-1)
    return x

_drawn_inputs = setup_inputs


def setup_inputs(seed=0):
    import zlib

    import numpy as np

    out = dict(_drawn_inputs(seed))
    spreads = {'L1_gnn_ln_w': (1.0, 0.2), 'L1_gnn_ln_b': (0.0, 0.1)}
    factors = {}
    for name, (base, spread) in spreads.items():
        noise = np.random.default_rng([zlib.crc32(name.encode()), seed]).standard_normal(out[name].shape)
        drawn = base * np.exp(spread * noise) if base else spread * noise
        out[name] = jnp.asarray(drawn.astype(out[name].dtype))
    for name, factor in factors.items():
        out[name] = (out[name] * factor).astype(out[name].dtype)
    return out
```

```python
import math
from contextlib import ExitStack

import concourse.bass as bass
from concourse import mybir
from concourse.alu_op_type import AluOpType as ALU

F32 = mybir.dt.float32
I32 = mybir.dt.int32
ACT = mybir.ActivationFunctionType
AX = mybir.AxisListType.X

P = 128
NODES = 12500
EDGES = 212500
FEAT = 256
MUL = 64
SCALARS = 8
HEADS = 8
HEAD_DIM = FEAT // HEADS
BATCH = 7
BATCHES = 2 * math.ceil(NODES / P / BATCH / 2)
NODE_TILES = BATCHES * BATCH
NODES_PAD = NODE_TILES * P
TILES = 14
HALF = TILES // 2
GROUP = TILES * P
GROUPS = 2 * math.ceil(EDGES / GROUP / 2)
EDGES_PAD = GROUPS * GROUP
PER_ROW = EDGES_PAD // P
WINDOW = 128
TABLE = NODES_PAD + WINDOW
ROUNDS = math.ceil(NODES_PAD / WINDOW)
ROUND_BLOCK = 14
BANKS = 4
AHEAD = 3
HIDDEN_AT, COPY_AT, ADD_AT = 7, 1, 4

NEG = -1e30
SILU_NORM = 1.679
LN_EPS = 1e-5
SOFTMAX_EPS = 1e-16
NEG_SLOPE = 0.2
C_S = math.sin(math.pi / 8.0)
C_X = math.cos(math.pi / 8.0)
CONV_SCALE = C_X / math.sqrt(20.0) / math.sqrt(2 * MUL)
SELF_SCALE = C_S / math.sqrt(MUL)


def in_pairs(eng, steps, body, peeled=1):
    for i in range(peeled):
        body(i, i == 0, False)
    with eng.Fori(peeled, steps // 2 - 1) as i:
        body(i, False, False)
    body(steps // 2 - 1, False, True)


def is_pair(i, n):
    return type(i) is int and i == n


def wait_alone(eng, sem, value):
    eng.wait_ge(sem, value)
    eng.nop(nofuse=True)


class Phase:

    def __init__(self, nc, name):
        self.nc, self.name, self.stack, self.sems = nc, name, ExitStack(), []

    def __enter__(self):
        self.stack.__enter__()
        return self

    def __exit__(self, *e):
        if e[0] is None:
            self.clear()
        return self.stack.__exit__(*e)

    def sb(self, name, shape, dt=F32):
        return self.stack.enter_context(self.nc.sbuf_tensor(f"{self.name}_{name}", shape, dt))

    def ps(self, name, shape, dt=F32):
        return self.stack.enter_context(self.nc.psum_tensor(f"{self.name}_{name}", shape, dt))

    def sem(self, name):
        s = self.stack.enter_context(self.nc.semaphore(f"{self.name}_{name}"))
        self.sems.append(s)
        return s

    def clear(self):
        self.nc.gpsimd.dma_reset()
        for s in self.sems:
            self.nc.gpsimd.sem_clear(s)
        self.nc.all_engine_barrier()


def constants(nc, io, c):
    with Phase(nc, "const") as ph:
        loaded, ramped, zeroed, made = ph.sem("loaded"), ph.sem("ramped"), ph.sem("zeroed"), ph.sem("made")
        ones = ph.sb("ones", [P, P])
        with nc.Block() as block:
            @block.sync
            def _(sp):
                sp.dma_start(c["factor"][:], io["node_factor"]).then_inc(loaded, 16)
                with nc.allow_non_contiguous_dma(reason="one destination of each group"):
                    per_group = io["dst"].rearrange("(o g e) -> o g e", o=1, e=GROUP)
                    sp.dma_start(c["first_dst"][:], per_group[:, :, 0]).then_inc(loaded, 16)
                    sp.dma_start(c["last_dst"][:], per_group[:, :, GROUP - 1]).then_inc(loaded, 16)
                sp.wait_ge(loaded, 48)

            @block.gpsimd
            def _(pool):
                nc.gpsimd.iota(c["ramp"][:], [[1, WINDOW]], base=0, channel_multiplier=0,
                               allow_small_or_imprecise_dtypes=True).then_inc(ramped, 1)
                nc.gpsimd.memset(ones[:], 1.0).then_inc(zeroed, 1)
                pool.wait_ge(zeroed, 1)
                nc.gpsimd.affine_select(out=c["ident"][:], in_=ones[:], compare_op=ALU.is_equal, fill=0.0,
                                        base=0, pattern=[[-1, P]], channel_multiplier=1).then_inc(ramped, 1)
                pool.wait_ge(ramped, 2)

            @block.vector
            def _(dve):
                nc.vector.memset(c["one_row"][:], 1.0).then_inc(made, 1)
                nc.vector.memset(c["ln_eps"][:], LN_EPS).then_inc(made, 1)
                dve.wait_ge(loaded, 48)
                nc.vector.tensor_tensor(c["reach"][:], c["last_dst"][:], c["first_dst"][:],
                                        ALU.subtract).then_inc(made, 1)
                dve.wait_ge(made, 3)
                nc.vector.tensor_reduce(c["span_f"][:], c["reach"][:], AX, ALU.max).then_inc(made, 1)
                dve.wait_ge(made, 4)
                nc.vector.tensor_copy(c["span"][:], c["span_f"][:]).then_inc(made, 1)
                nc.vector.tensor_scalar(c["factor8"][:], c["factor"][:], 1.0 / math.sqrt(MUL), None,
                                        ALU.mult).then_inc(made, 1)


def batch_rows(table, s):
    return table[bass.ds(s * BATCH * P, BATCH * P), :].rearrange("(p j) f -> p (j f)", p=P)


def block_matrix(dma, sem, tile, blocks):
    for r, q, w in blocks:
        dma.dma_start(tile[MUL * r:MUL * r + MUL, MUL * q:MUL * q + MUL], w).then_inc(sem, 16)


def project_sources(nc, io, c, y, tables):
    with Phase(nc, "lin1") as ph:
        w = ph.sb("w", [P, 2, P])
        zeros = ph.sb("zeros", [P, 4096])
        xt = ph.sb("xt", [P, 2, 2, BATCH, P])
        yb = ph.sb("yb", [P, 2, BATCH, FEAT])
        acc = [ph.ps(f"acc{k}", [P, 512]) for k in range(BATCH)]
        zeroed, w_in, cleared = ph.sem("zeroed"), ph.sem("w_in"), ph.sem("cleared")
        x_in = [ph.sem(f"x_in{b}") for b in range(2)]
        y_out = [ph.sem(f"y_out{b}") for b in range(2)]
        product, scaled = ph.sem("product"), ph.sem("scaled")
        xt_dram = io["x_t"].rearrange("(c f) n -> f c n", c=2)

        with nc.Block() as block:
            @block.sync
            def _(sp):
                def load(s, b):
                    sp.dma_start(xt[:, b].rearrange("p c j n -> p c (j n)"),
                                 xt_dram[:, :, bass.ds(s * BATCH * P, BATCH * P)]).then_inc(x_in[b], 16)

                def pair(i, first, last):
                    if first:
                        load(0, 0)
                        load(1, 1)
                    for b in range(2):
                        s = 2 * i + b
                        wait_alone(sp, scaled, BATCH * (s + 1))
                        sp.dma_start(batch_rows(y, s), yb[:, b].rearrange("p j f -> p (j f)")).then_inc(y_out[b], 16)
                        if not last:
                            load(s + 2, b)

                sp.wait_ge(zeroed, 2)
                w0, w1 = io["lin1_w0"], io["lin1_w1"]
                block_matrix(sp, w_in, w[:, 0, :], [(0, 0, w0), (1, 1, w1)])
                block_matrix(sp, w_in, w[:, 1, :], [(0, 0, w1), (1, 1, w1)])
                in_pairs(sp, BATCHES, pair)
                for b in range(2):
                    sp.wait_ge(y_out[b], 16 * BATCHES // 2)

            @block.vector
            def _(dve):
                nc.vector.memset(w[:], 0.0).then_inc(zeroed, 1)
                nc.vector.memset(zeros[:], 0.0).then_inc(zeroed, 1)

            @block.gpsimd
            def _(pool):
                pool.wait_ge(zeroed, 2)
                n = 0
                for table in tables:
                    rows = table.rearrange("(p r) f -> p (r f)", p=P)
                    width = rows.shape[1]
                    for at in range(0, width, 4096):
                        size = min(4096, width - at)
                        pool.dma_start(rows[:, at:at + size], zeros[:, 0:size]).then_inc(cleared, 16)
                        n += 1
                pool.wait_ge(cleared, 16 * n)

            @block.tensor
            def _(pe):
                pe.wait_ge(w_in, 16 * 4)

                def pair(i, first, last):
                    for b in range(2):
                        s = 2 * i + b
                        pe.wait_ge(x_in[b], 16 * (i + 1))
                        for k in range(BATCH):
                            if not (first and b == 0):
                                pe.wait_ge(scaled, BATCH * (s - 1) + k + 1)
                            for h in range(2):
                                mm = nc.tensor.matmul(acc[k][:, h * P:(h + 1) * P], xt[:, b, h, k], w[:, h, :],
                                                      start=True, stop=True, skip_group_check=True)
                            mm.then_inc(product, 1)
                in_pairs(pe, BATCHES, pair)

            @block.scalar
            def _(act):
                def pair(i, first, last):
                    for b in range(2):
                        s = 2 * i + b
                        if not first:
                            act.wait_ge(y_out[b], 16 * i)
                        for k in range(BATCH):
                            act.wait_ge(product, BATCH * s + k + 1)
                            nc.scalar.activation(yb[:, b, k], acc[k][:, 0:FEAT], ACT.Copy,
                                                 scale=c["factor8"][:, bass.ds(BATCH * s + k, 1)])\
                                .then_inc(scaled, 1)
                in_pairs(act, BATCHES, pair)


def rounds(nc, c, body):
    span = nc.values_load(c["span"][0:1, 0:1], min_val=0, max_val=NODES_PAD)
    with nc.Fori(0, math.ceil(ROUNDS / ROUND_BLOCK)) as a:
        with nc.If(a * (ROUND_BLOCK * WINDOW) <= span):
            with nc.Fori(0, ROUND_BLOCK) as r:
                with nc.If((a * ROUND_BLOCK + r) * WINDOW <= span):
                    body()
                with nc.Else():
                    nc.all_engine_barrier()
        with nc.Else():
            nc.all_engine_barrier()


def place_windows(nc, c, ph, bcast):
    clamped, moved, spread, copied = ph.sem("clamped"), ph.sem("moved"), ph.sem("spread"), ph.sem("copied")

    def run():
        with nc.Block() as block:
            @block.vector
            def _(dve):
                nc.vector.tensor_scalar(c["start_f"][:], c["shift"][:], float(NODES_PAD), None,
                                        ALU.min).then_inc(clamped, 1)
                dve.wait_ge(clamped, 1)
                nc.vector.tensor_copy(c["start_i"][:], c["start_f"][:]).then_inc(moved, 1)
                nc.vector.tensor_scalar(c["shift"][:], c["shift"][:], float(WINDOW), None,
                                        ALU.add).then_inc(moved, 1)
                dve.wait_ge(spread, 1)
                nc.vector.tensor_copy(c["start_b"][:], bcast[:, 0:GROUPS]).then_inc(copied, 1)

            @block.tensor
            def _(pe):
                pe.wait_ge(clamped, 1)
                nc.tensor.matmul(bcast[:, 0:GROUPS], c["one_row"][:], c["start_f"][:],
                                 start=True, stop=True).then_inc(spread, 1)
    return run


def start_windows(nc, c, name):
    with Phase(nc, name) as ph:
        done = ph.sem("done")
        with nc.Block() as block:
            @block.vector
            def _(dve):
                nc.vector.tensor_copy(c["shift"][:], c["first_dst"][:]).then_inc(done, 1)


def convolve_edges(nc, io, c, y, sums):
    with Phase(nc, "conv") as ph:
        fc1 = ph.sb("fc1", [P, P])
        fc2 = ph.sb("fc2", [P, 2, 4 * MUL])
        es = ph.sb("es", [P, 2, HALF * P])
        ids = ph.sb("ids", [P, 2, 2 * TILES], I32)
        ea = ph.sb("ea", [P, 2, TILES * 4])
        ht = ph.sb("ht", [P, 2, HALF, P])
        xg = ph.sb("xg", [P, 2, TILES, FEAT])
        rel = ph.sb("rel", [P, TILES])
        sel = ph.sb("sel", [P, 2, TILES, WINDOW])
        dots = ph.sb("dots", [P, HALF, 3, MUL])
        dot = ph.sb("dot", [P, 2, HALF, MUL])
        raw = ph.sb("raw", [P, HALF, 5, MUL])
        mids = ph.sb("mids", [P, HALF, 8, MUL])
        agg_s = ph.sb("agg_s", [P, 2, 8 * MUL])
        psum_h = [ph.ps(f"h{b}", [P, 512]) for b in range(2)]
        psum_w = [ph.ps(f"w{n}", [P, 8, MUL]) for n in range(BANKS)]
        psum_a = [ph.ps(f"a{b}", [P, 512]) for b in range(2)]
        zeroed, weights_in, scaled = ph.sem("zeroed"), ph.sem("weights_in"), ph.sem("scaled")

        with nc.Block() as block:
            @block.vector
            def _(dve):
                nc.vector.memset(fc1[:], 0.0).then_inc(zeroed, 1)
                nc.vector.memset(fc2[:], 0.0).then_inc(zeroed, 1)
                nc.vector.memset(es[:], 0.0).then_inc(zeroed, 1)
                dve.wait_ge(weights_in, 16 * 4)
                nc.vector.tensor_scalar(fc2[:], fc2[:], SILU_NORM / math.sqrt(MUL), None,
                                        ALU.mult).then_inc(scaled, 1)
                dve.wait_ge(scaled, 1)
                nc.vector.tensor_scalar(fc2[:, :, MUL:2 * MUL], fc2[:, :, MUL:2 * MUL], 1.0 / math.sqrt(3.0), None,
                                        ALU.mult).then_inc(scaled, 1)

            @block.sync
            def _(sp):
                sp.wait_ge(zeroed, 3)
                for h in range(2):
                    sp.dma_start(fc1[h * SCALARS:(h + 1) * SCALARS, h * MUL:(h + 1) * MUL], io["fc_w1"])\
                        .then_inc(weights_in, 16)
                    sp.dma_start(fc2[h * MUL:(h + 1) * MUL, h], io["fc_w2"]).then_inc(weights_in, 16)
                sp.wait_ge(weights_in, 16 * 4)

        with Phase(nc, "conv_r") as rs:
            place = place_windows(nc, c, rs, psum_a[0])
            meta_in = [rs.sem(f"meta_in{b}") for b in range(2)]
            rows_in = [[rs.sem(f"rows_in{b}_{k}") for k in range(TILES)] for b in range(2)]
            h_done, silu_done, w_done = rs.sem("h_done"), rs.sem("silu_done"), rs.sem("w_done")
            rel_done, sel_done, dots_done, dot_part = (rs.sem(n) for n in ("rel", "sel", "dots", "dot_part"))
            dot_done, c_done, raw_done = rs.sem("dot_done"), rs.sem("c_done"), rs.sem("raw_done")
            ad_done, mids_done, agg_done = rs.sem("ad_done"), rs.sem("mids_done"), rs.sem("agg_done")
            copied, added = rs.sem("agg_copied"), rs.sem("added")

            def one_round():
                place()
                with nc.Block() as block:
                    @block.sync
                    def _(sp):
                        def pair(i, first, last):
                            for b in range(2):
                                g = 2 * i + b
                                if not first:
                                    wait_alone(sp, h_done, g - 1)
                                    wait_alone(sp, ad_done, TILES * (g - 1))
                                    wait_alone(sp, mids_done, TILES * (g - 1))
                                sp.dma_start(ids[:, b], io["ids"][bass.ds(g, 1)].rearrange("o p k -> (o p) k"))\
                                    .then_inc(meta_in[b], 16)
                                sp.dma_start(ea[:, b], io["edge_attr"][bass.ds(g, 1)]
                                             .rearrange("o p k -> (o p) k")).then_inc(meta_in[b], 16)
                                sp.dma_start(es[0:2 * SCALARS, b],
                                             io["edge_scalars_t"][:, bass.ds(g * HALF * P, HALF * P)])\
                                    .then_inc(meta_in[b], 16)
                        in_pairs(sp, GROUPS, pair)

                    @block.gpsimd
                    def _(pool):
                        def add_sums(g, b, first):
                            wait_alone(pool, copied, g + 1)
                            if not first:
                                wait_alone(pool, added, 16 * g)
                            at = pool.value_load(c["start_i"][0:1, bass.ds(g, 1)], min_val=0, max_val=NODES_PAD)
                            pool.dma_start(sums[bass.ds(at, WINDOW), :], agg_s[:, b], accum_op=ALU.add)\
                                .then_inc(added, 16)

                        def pair(i, first, last):
                            for b in range(2):
                                g = 2 * i + b
                                wait_alone(pool, meta_in[b], 48 * (i + 1))
                                for k in range(TILES):
                                    if not first:
                                        wait_alone(pool, mids_done, TILES * (g - 2) + k + 1)
                                    nc.gpsimd.indirect_dma_start(
                                        xg[:, b, k], None, y,
                                        bass.IndirectOffsetOnAxis(ids[:, b, k:k + 1], 0))\
                                        .then_inc(rows_in[b][k], 16)
                                    if k == ADD_AT and not first:
                                        add_sums(g - 2, b, b == 0 and is_pair(i, 1))
                            if last:
                                add_sums(GROUPS - 2, 0, False)
                                add_sums(GROUPS - 1, 1, False)
                                pool.wait_ge(added, 16 * GROUPS)

                        in_pairs(pool, GROUPS, pair, 2)
                        for b in range(2):
                            for k in range(TILES):
                                pool.wait_ge(rows_in[b][k], 16 * GROUPS // 2)

                    @block.tensor
                    def _(pe):
                        def hidden(g, b, i, first):
                            pe.wait_ge(meta_in[b], 48 * (i + 1))
                            if not first:
                                pe.wait_ge(silu_done, g)
                            half = HALF * P // 2
                            for q in range(2):
                                mm = nc.tensor.matmul(psum_h[q][:, 0:half], fc1[:],
                                                      es[:, b, q * half:(q + 1) * half], start=True, stop=True)
                            mm.then_inc(h_done, 1)

                        def weigh(g, b, k, t, first):
                            pe.wait_ge(silu_done, g + 1)
                            if not first:
                                pe.wait_ge(mids_done, t - BANKS + 1)
                            nc.tensor.matmul(psum_w[(TILES * b + k) % BANKS][:, 0:4].rearrange("p q f -> p (q f)"),
                                             ht[:, b, k % HALF], fc2[:, k // HALF], start=True, stop=True,
                                             skip_group_check=True).then_inc(w_done, 1)

                        def pair(i, first, last):
                            if first:
                                hidden(0, 0, 0, True)
                                for k in range(AHEAD):
                                    weigh(0, 0, k, k, True)
                            for b in range(2):
                                g = 2 * i + b
                                last_g = last and b == 1
                                for k in range(TILES):
                                    t = TILES * g + k
                                    if k == HIDDEN_AT and not last_g:
                                        hidden(g + 1, 1 - b, i + b, False)
                                    ahead = k + AHEAD
                                    if ahead < TILES:
                                        weigh(g, b, ahead, t + AHEAD, first and b == 0 and ahead < BANKS)
                                    elif not last_g:
                                        weigh(g + 1, 1 - b, ahead - TILES, t + AHEAD, False)
                                    if k == 0:
                                        pe.wait_ge(sel_done, 2 * g + 2)
                                        if not first:
                                            pe.wait_ge(copied, g - 1)
                                    pe.wait_ge(mids_done, t + 1)
                                    pe.wait_ge(ad_done, t + 1)
                                    nc.tensor.matmul(psum_a[b][:], sel[:, b, k],
                                                     mids[:, k % HALF].rearrange("p q f -> p (q f)"),
                                                     start=(k == 0), stop=(k == TILES - 1)).then_inc(agg_done, 1)
                        in_pairs(pe, GROUPS, pair)

                    @block.scalar
                    def _(act):
                        def silu(g, b, first):
                            act.wait_ge(h_done, g + 1)
                            if not first:
                                act.wait_ge(w_done, TILES * (g - 1))
                            flat = ht[:, b].rearrange("f k p -> f (k p)")
                            half = HALF * P // 2
                            for q in range(2):
                                a = nc.scalar.activation(flat[:, q * half:(q + 1) * half], psum_h[q][:, 0:half],
                                                         ACT.Silu, scale=1.0 / math.sqrt(SCALARS))
                            a.then_inc(silu_done, 1)

                        def copy_out(g, b, first):
                            act.wait_ge(agg_done, TILES * (g + 1))
                            if not first:
                                act.wait_ge(added, 16 * (g - 1))
                            nc.scalar.activation(agg_s[:, b], psum_a[b][:], ACT.Copy).then_inc(copied, 1)

                        def pair(i, first, last):
                            if first:
                                silu(0, 0, True)
                            for b in range(2):
                                g = 2 * i + b
                                for k in range(TILES):
                                    if k == HIDDEN_AT + 1 and not (last and b == 1):
                                        silu(g + 1, 1 - b, first and b == 0)
                                    if k == COPY_AT and not (first and b == 0):
                                        copy_out(g - 1, 1 - b, first or (b == 0 and is_pair(i, 1)))
                                    act.wait_ge(raw_done, TILES * g + k + 1)
                                    s = k % HALF
                                    nc.scalar.activation(mids[:, s, 0:4], raw[:, s, 0:4], ACT.Copy,
                                                         scale=ea[:, b, 4 * k:4 * k + 1]).then_inc(ad_done, 1)
                            if last:
                                copy_out(GROUPS - 1, 1, False)
                        in_pairs(act, GROUPS, pair, 2)

                    @block.vector
                    def _(dve):
                        def select(g, b, i, half, first):
                            if half == 0:
                                dve.wait_ge(meta_in[b], 48 * (i + 1))
                                nc.vector.tensor_scalar(rel[:], ids[:, b, TILES:2 * TILES],
                                                        c["start_b"][:, bass.ds(g, 1)], None,
                                                        ALU.subtract).then_inc(rel_done, 1)
                                dve.wait_ge(rel_done, g + 1)
                                if not first:
                                    dve.wait_ge(agg_done, TILES * (g - 1))
                            part = slice(half * HALF, (half + 1) * HALF)
                            shape = [P, HALF, WINDOW]
                            nc.vector.tensor_tensor(
                                sel[:, b, part], rel[:, part].unsqueeze(2).to_broadcast(shape),
                                c["ramp"][:].unsqueeze(1).to_broadcast(shape), ALU.is_equal).then_inc(sel_done, 1)

                        def dot_products(g, b, i, half):
                            n = 2 * g + half
                            for k in range(half * HALF, (half + 1) * HALF):
                                dve.wait_ge(rows_in[b][k], 16 * (i + 1))
                            shape = [P, HALF, 3, MUL]
                            part = slice(half * HALF, (half + 1) * HALF)
                            e = ea[:, b].rearrange("p (k f) -> p k f", f=4)[:, part, 1:4]
                            nc.vector.tensor_tensor(
                                dots[:], xg[:, b, part, MUL:].rearrange("p k (c f) -> p k c f", c=3),
                                e.unsqueeze(3).to_broadcast(shape), ALU.mult).then_inc(dots_done, 1)
                            dve.wait_ge(dots_done, n + 1)
                            nc.vector.tensor_tensor(dot[:, half], dots[:, :, 0], dots[:, :, 1],
                                                    ALU.add).then_inc(dot_part, 1)
                            dve.wait_ge(dot_part, n + 1)
                            nc.vector.tensor_tensor(dot[:, half], dot[:, half], dots[:, :, 2],
                                                    ALU.add).then_inc(dot_done, 1)

                        def pair(i, first, last):
                            if first:
                                select(0, 0, 0, 0, True)
                                select(0, 0, 0, 1, True)
                                dot_products(0, 0, 0, 0)
                            for b in range(2):
                                g = 2 * i + b
                                last_g = last and b == 1
                                for k in range(TILES):
                                    t = TILES * g + k
                                    s = k % HALF
                                    dve.wait_ge(w_done, t + 1)
                                    if not (first and b == 0 and k < HALF):
                                        dve.wait_ge(agg_done, t - HALF + 1)
                                    w = psum_w[(TILES * b + k) % BANKS]
                                    m, x = mids[:, s], xg[:, b, k].rearrange("p (c f) -> p c f", c=4)
                                    nc.vector.tensor_tensor(raw[:, s, 0::4], w[:, 0:4:2],
                                                            x[:, 0:1].to_broadcast([P, 2, MUL]),
                                                            ALU.mult).then_inc(c_done, 1)
                                    nc.vector.tensor_tensor(raw[:, s, 1:4], w[:, 3:4].to_broadcast([P, 3, MUL]),
                                                            x[:, 1:4], ALU.mult).then_inc(raw_done, 1)
                                    if k % HALF == 0:
                                        dve.wait_ge(dot_done, 2 * g + k // HALF + 1)
                                    nc.vector.tensor_tensor(m[:, 7], w[:, 1], dot[:, k // HALF, s], ALU.mult)
                                    dve.wait_ge(c_done, t + 1)
                                    nc.vector.tensor_tensor(
                                        m[:, 4:7], raw[:, s, 4:5].to_broadcast([P, 3, MUL]),
                                        ea[:, b, 4 * k + 1:4 * k + 4].unsqueeze(2).to_broadcast([P, 3, MUL]),
                                        ALU.mult).then_inc(mids_done, 1)
                                    if k == 4:
                                        dot_products(g, b, i, 1)
                                    if k in (6, 8) and not last_g:
                                        select(g + 1, 1 - b, i + b, (k - 6) // 2, first and b == 0)
                                    if k == 11 and not last_g:
                                        dot_products(g + 1, 1 - b, i + b, 0)
                        in_pairs(dve, GROUPS, pair)
                rs.clear()
            rounds(nc, c, one_round)


def end_convolution(nc, io, c, sums, x1, xpa, att):
    TURN = 2 * BATCH - 1
    PAIR = 2 * BATCH
    with Phase(nc, "mid") as ph:
        w_self = ph.sb("w_self", [P, 2, P])
        w_self_raw = ph.sb("w_self_raw", [P, 2, P])
        lin2_raw = ph.sb("lin2_raw", [P, 6, P])
        lin2 = ph.sb("lin2", [P, 6, P])
        w_proj = ph.sb("w_proj", [P, 2, FEAT + 2 * HEADS])
        w_proj_t = ph.sb("w_proj_t", [P, 2, FEAT])
        w_att = ph.sb("w_att", [P, 2, 2 * HEADS])
        att_zero = ph.sb("att_zero", [WINDOW, 2 * HEADS])
        xt = ph.sb("xt", [P, 2, 2, BATCH, P])
        xn = ph.sb("xn", [P, 2, BATCH, FEAT])
        rows = ph.sb("rows", [P, 2, BATCH, 4, P])
        rows_t = ph.sb("rows_t", [P, 2, 4, P])
        pre = ph.sb("pre", [P, 2, BATCH, FEAT])
        stats = ph.sb("stats", [P, 2, BATCH, 6])
        mean_var = ph.sb("mean_var", [P, 2, BATCH, 2])
        std = ph.sb("std", [P, 2, BATCH])
        rstd = ph.sb("rstd", [P, 2, BATCH])
        out = ph.sb("out", [P, 2, BATCH, FEAT])
        out_t = ph.sb("out_t", [P, 2, 2, P])
        proj = ph.sb("proj", [P, 2, BATCH, FEAT + HEADS])
        proj_a = ph.sb("proj_a", [P, 2, BATCH, 2 * HEADS])
        psum_s = [ph.ps(f"s{b}", [P, 4, P]) for b in range(2)]
        psum_z = [ph.ps(f"z{b}", [P, 512]) for b in range(2)]
        psum_t = [ph.ps(f"t{b}", [P, 512]) for b in range(2)]
        psum_p = [ph.ps(f"p{b}", [P, 512]) for b in range(2)]
        zeroed, w_in, w_made, att_out = ph.sem("zeroed"), ph.sem("w_in"), ph.sem("w_made"), ph.sem("att_out")
        x_in = [ph.sem(f"x_in{b}") for b in range(2)]
        stored = [ph.sem(f"stored{b}") for b in range(2)]
        proj_stored = [ph.sem(f"proj_stored{b}") for b in range(2)]
        s_turned, s_copied, z_done, pre_done = (ph.sem(n) for n in ("s_turned", "s_copied", "z_done", "pre_done"))
        stat_done, aggr_done = ph.sem("stat_done"), ph.sem("aggr_done")
        std_done, rstd_done, out_done = ph.sem("std_done"), ph.sem("rstd_done"), ph.sem("out_done")
        t_done, t_copied, p_done, p_copied = ph.sem("t_done"), ph.sem("t_copied"), ph.sem("p_done"), ph.sem("p_copied")
        att_done = ph.sem("att_done")
        xt_dram = io["x_t"].rearrange("(c f) n -> f c n", c=2)

        with nc.Block() as block:
            @block.sync
            def _(sp):
                sp.dma_start(w_proj[:, :, 0:FEAT], io["lin_w"].rearrange("(c f) n -> f c n", c=2)).then_inc(w_in, 16)
                sp.dma_start(w_proj_t[:], io["lin_w_t"].rearrange("(c f) n -> f c n", c=2)).then_inc(w_in, 16)
                sp.wait_ge(zeroed, 4)
                w0, w1 = io["sc_w0"], io["sc_w1"]
                block_matrix(sp, w_in, w_self_raw[:, 0, :], [(0, 0, w0), (1, 1, w1)])
                block_matrix(sp, w_in, w_self_raw[:, 1, :], [(0, 0, w1), (1, 1, w1)])
                w00, w01, w10, w11 = (io[f"lin2_w{n}"] for n in ("00", "01", "10", "11"))
                block_matrix(sp, w_in, lin2_raw[:, 0, :], [(0, 0, w00), (1, 1, w11)])
                block_matrix(sp, w_in, lin2_raw[:, 1, :], [(0, 0, w11), (1, 1, w11)])
                block_matrix(sp, w_in, lin2_raw[:, 2, :], [(0, 1, w10)])
                block_matrix(sp, w_in, lin2_raw[:, 3, :], [(1, 0, w10)])
                block_matrix(sp, w_in, lin2_raw[:, 4, :], [(1, 0, w01)])
                block_matrix(sp, w_in, lin2_raw[:, 5, :], [(0, 1, w10)])
                sp.dma_start(att[NODES_PAD:TABLE, :], att_zero[:]).then_inc(att_out, 16)
                with nc.allow_non_contiguous_dma(reason="columns of the attention's block matrix, once"):
                    for h in range(HEADS):
                        at = h * HEAD_DIM % P
                        part = w_att[at:at + HEAD_DIM, h * HEAD_DIM // P, :]
                        sp.dma_start(part[:, h:h + 1], io["att_t"][HEAD_DIM:2 * HEAD_DIM, h:h + 1]).then_inc(w_in, 16)
                        sp.dma_start(part[:, HEADS + h:HEADS + h + 1], io["att_t"][0:HEAD_DIM, h:h + 1])\
                            .then_inc(w_in, 16)
                sp.wait_ge(att_out, 16)

            @block.vector
            def _(dve):
                nc.vector.memset(w_self_raw[:], 0.0).then_inc(zeroed, 1)
                nc.vector.memset(lin2_raw[:], 0.0).then_inc(zeroed, 1)
                nc.vector.memset(w_att[:], 0.0).then_inc(zeroed, 1)
                nc.vector.memset(att_zero[:], 0.0).then_inc(zeroed, 1)
                dve.wait_ge(w_in, 16 * (14 + 2 * HEADS))
                nc.vector.tensor_scalar(w_self[:], w_self_raw[:], SELF_SCALE, None, ALU.mult).then_inc(w_made, 1)
                nc.vector.tensor_scalar(lin2[:], lin2_raw[:], CONV_SCALE, None, ALU.mult).then_inc(w_made, 1)
                for r in range(2):
                    dve.wait_ge(att_done, r + 1)
                    nc.vector.tensor_copy(w_proj[:, r, FEAT:FEAT + 2 * HEADS], psum_z[r][:, 0:2 * HEADS])\
                        .then_inc(w_made, 1)

            @block.tensor
            def _(pe):
                pe.wait_ge(w_in, 16 * (14 + 2 * HEADS))
                for r in range(2):
                    for h in range(2):
                        last = nc.tensor.matmul(psum_z[r][:, 0:2 * HEADS], w_proj_t[:, h, r * P:(r + 1) * P],
                                                w_att[:, h], start=(h == 0), stop=(h == 1))
                    last.then_inc(att_done, 1)

        def steps(i, first, last, step):
            for n in range(PAIR + TURN + 2 if last else PAIR):
                step(PAIR * i + n, n,
                     lambda d: not (type(i) is int and PAIR * i + n < d) and not (last and n - d >= PAIR))

        def place_of(n):
            return n % PAIR // BATCH, n % BATCH

        with nc.Block() as block:
            @block.sync
            def _(sp):
                def load(s, b):
                    sp.dma_start(rows[:, b].rearrange("p j q f -> p (j q f)"), batch_rows(sums, s))\
                        .then_inc(x_in[b], 16)
                    sp.dma_start(xt[:, b].rearrange("p c j n -> p c (j n)"),
                                 xt_dram[:, :, bass.ds(s * BATCH * P, BATCH * P)]).then_inc(x_in[b], 16)
                    sp.dma_start(xn[:, b].rearrange("p j f -> p (j f)"), batch_rows(io["x"], s)).then_inc(x_in[b], 16)

                def store_proj(s, b):
                    wait_alone(sp, p_copied, BATCH * (s + 1))
                    sp.dma_start(batch_rows(xpa, s), proj[:, b].rearrange("p j f -> p (j f)"))\
                        .then_inc(proj_stored[b], 16)
                    sp.dma_start(batch_rows(att, s), proj_a[:, b].rearrange("p j f -> p (j f)"))\
                        .then_inc(proj_stored[b], 16)

                def pair(i, first, last):
                    if first:
                        load(0, 0)
                        load(1, 1)
                    for b in range(2):
                        s = 2 * i + b
                        if not last:
                            wait_alone(sp, pre_done, BATCH * (s + 1))
                            load(s + 2, b)
                        wait_alone(sp, out_done, BATCH * (s + 1))
                        sp.dma_start(batch_rows(x1, s), out[:, b].rearrange("p j f -> p (j f)")).then_inc(stored[b], 16)
                        if not (first and b == 0):
                            store_proj(s - 1, 1 - b)
                    if last:
                        store_proj(BATCHES - 1, 1)
                in_pairs(sp, BATCHES, pair)
                for b in range(2):
                    sp.wait_ge(stored[b], 16 * BATCHES // 2)
                    sp.wait_ge(proj_stored[b], 32 * BATCHES // 2)

            @block.tensor
            def _(pe):
                def pair(i, first, last):
                    def step(t, n, exists):
                        if exists(0):
                            b, j = place_of(n)
                            if j == 0:
                                pe.wait_ge(x_in[b], 48 * (i + 1))
                            if exists(2):
                                pe.wait_ge(s_copied, t - 1)
                            for q in range(4):
                                mm = nc.tensor.transpose(psum_s[n % 2][:, q], rows[:, b, j, q], c["ident"][:])
                            mm.then_inc(s_turned, 1)
                        if exists(1):
                            b, j = place_of(n - 1)
                            r = (n - 1) % 2
                            pe.wait_ge(s_copied, t)
                            if exists(3):
                                pe.wait_ge(pre_done, t - 2)
                            z = psum_z[r]
                            for q in (2, 3):
                                nc.tensor.matmul(z[:, 0:FEAT], rows_t[:, r, q],
                                                 lin2[:, 2 * q - 2:2 * q].rearrange("p h f -> p (h f)"),
                                                 start=(q == 2), stop=False, skip_group_check=True)
                            for h in range(2):
                                nc.tensor.matmul(z[:, h * P:(h + 1) * P], rows_t[:, r, h], lin2[:, h],
                                                 start=False, stop=False, skip_group_check=True)
                                mm = nc.tensor.matmul(z[:, h * P:(h + 1) * P], xt[:, b, h, j], w_self[:, h],
                                                      start=False, stop=True, skip_group_check=True)
                            mm.then_inc(z_done, 1)
                        if exists(TURN):
                            b, j = place_of(n - TURN)
                            r = (n - TURN) % 2
                            pe.wait_ge(out_done, t - TURN + 1)
                            if exists(TURN + 2):
                                pe.wait_ge(t_copied, t - TURN - 1)
                            for h in range(2):
                                mm = nc.tensor.transpose(psum_t[r][:, h * P:(h + 1) * P],
                                                         out[:, b, j, h * P:(h + 1) * P], c["ident"][:])
                            mm.then_inc(t_done, 1)
                        if exists(TURN + 1):
                            r = (n - TURN - 1) % 2
                            pe.wait_ge(t_copied, t - TURN)
                            if exists(TURN + 3):
                                pe.wait_ge(p_copied, t - TURN - 2)
                            for h in range(2):
                                mm = nc.tensor.matmul(psum_p[r][:, 0:FEAT + 2 * HEADS], out_t[:, r, h], w_proj[:, h],
                                                      start=(h == 0), stop=(h == 1))
                            mm.then_inc(p_done, 1)
                    steps(i, first, last, step)
                in_pairs(pe, BATCHES, pair, 2)

            @block.scalar
            def _(act):
                def pair(i, first, last):
                    def step(t, n, exists):
                        if exists(0):
                            act.wait_ge(s_turned, t + 1)
                            if exists(2):
                                act.wait_ge(z_done, t - 1)
                            nc.scalar.activation(rows_t[:, n % 2], psum_s[n % 2][:], ACT.Copy).then_inc(s_copied, 1)
                        if n % BATCH == 3 and exists(BATCH + 3):
                            b, _ = place_of(n - BATCH)
                            act.wait_ge(aggr_done, t - 3)
                            nc.scalar.activation(std[:, b], mean_var[:, b, :, 1], ACT.Sqrt, bias=c["ln_eps"][:])\
                                .then_inc(std_done, BATCH)
                        if exists(TURN):
                            r = (n - TURN) % 2
                            act.wait_ge(t_done, t - TURN + 1)
                            if exists(TURN + 2):
                                act.wait_ge(p_done, t - TURN - 1)
                            nc.scalar.activation(out_t[:, r], psum_t[r][:, 0:FEAT].rearrange("p (h n) -> p h n", h=2),
                                                 ACT.Copy).then_inc(t_copied, 1)
                        if exists(TURN + 1):
                            b, j = place_of(n - TURN - 1)
                            r = (n - TURN - 1) % 2
                            act.wait_ge(p_done, t - TURN)
                            if j == 0 and exists(TURN + 1 + PAIR):
                                act.wait_ge(proj_stored[b], 32 * (i + (n - TURN - 1) // PAIR))
                            nc.scalar.activation(proj[:, b, j], psum_p[r][:, 0:FEAT + HEADS], ACT.Copy)
                            nc.scalar.activation(proj_a[:, b, j], psum_p[r][:, FEAT:FEAT + 2 * HEADS], ACT.Copy)\
                                .then_inc(p_copied, 1)
                    steps(i, first, last, step)
                in_pairs(act, BATCHES, pair, 2)

            @block.vector
            def _(dve):
                def pair(i, first, last):
                    def step(t, n, exists):
                        if exists(1):
                            b, j = place_of(n - 1)
                            dve.wait_ge(z_done, t)
                            z, x, o = psum_z[(n - 1) % 2], xn[:, b, j], pre[:, b, j]
                            a = c["factor"][:, bass.ds(t - 1, 1)]
                            nc.vector.scalar_tensor_tensor(out=o[:, 0:MUL], in0=z[:, 0:MUL], scalar=a,
                                                           in1=x[:, 0:MUL], op0=ALU.mult, op1=ALU.add)
                            nc.vector.scalar_tensor_tensor(
                                out=o[:, MUL:].rearrange("p (u c) -> p c u", c=3),
                                in0=z[:, MUL:FEAT].rearrange("p (c u) -> p c u", c=3), scalar=a,
                                in1=x[:, MUL:].rearrange("p (u c) -> p c u", c=3), op0=ALU.mult,
                                op1=ALU.add).then_inc(pre_done, 1)
                        if exists(2):
                            b, j = place_of(n - 2)
                            dve.wait_ge(pre_done, t - 1)
                            nc.vector.bn_stats(stats[:, b, j], pre[:, b, j]).then_inc(stat_done, 1)
                        if n % BATCH == 2 and exists(BATCH + 2):
                            b, _ = place_of(n - BATCH)
                            wait_alone(dve, stat_done, t - 2)
                            for j in range(BATCH):
                                nc.vector.bn_aggr(mean_var[:, b, j], stats[:, b, j]).then_inc(aggr_done, 1)
                        if n % BATCH == 4 and exists(BATCH + 4):
                            b, _ = place_of(n - BATCH)
                            dve.wait_ge(std_done, t - 4)
                            nc.vector.reciprocal(rstd[:, b], std[:, b]).then_inc(rstd_done, BATCH)
                            dve.wait_ge(rstd_done, t - 4)
                            if exists(BATCH + 4 + PAIR):
                                dve.wait_ge(stored[b], 16 * (i + (n - BATCH) // PAIR))
                                dve.wait_ge(t_done, t - 4 - PAIR)
                            for j in range(BATCH):
                                nc.vector.tensor_scalar(out[:, b, j], pre[:, b, j], mean_var[:, b, j, 0:1],
                                                        rstd[:, b, j:j + 1], ALU.subtract,
                                                        ALU.mult).then_inc(out_done, 1)
                    steps(i, first, last, step)
                in_pairs(dve, BATCHES, pair, 2)


def source_maxima(nc, io, c, att, scores):
    with Phase(nc, "maxima") as ph:
        src = ph.sb("src", [P, PER_ROW], I32)
        dst = ph.sb("dst", [P, PER_ROW], I32)
        near = ph.sb("near", [P, PER_ROW], I32)
        starts = ph.sb("starts", [P, PER_ROW])
        ends = ph.sb("ends", [P, PER_ROW])
        own = ph.sb("own", [P, HEADS, PER_ROW])
        best = ph.sb("best", [P, HEADS, PER_ROW])
        idx = ph.sb("idx", [P, 2, TILES], I32)
        rows = ph.sb("rows", [P, 2, TILES, 2 * HEADS])
        tail = ph.sb("tail", [P, HEADS])
        broken = ph.sb("broken", [P, 1])
        broken8 = ph.sb("broken8", [P, HEADS])
        tail_t = ph.sb("tail_t", [HEADS, P])
        broken_t = ph.sb("broken_t", [HEADS, P])
        chain = ph.sb("chain", [HEADS, P])
        carry_t = ph.sb("carry_t", [HEADS, P])
        carry = ph.sb("carry", [P, HEADS])
        chunk = PER_ROW // TILES // 2
        packed = ph.sb("packed", [P, 2, chunk, 2 * HEADS])
        psum_t = ph.ps("t", [P, 512])
        psum_b = ph.ps("b", [P, 512])
        psum_c = ph.ps("c", [P, 512])
        src_in, dst_in = ph.sem("src_in"), ph.sem("dst_in")
        near_in, near_used = ph.sem("near_in"), ph.sem("near_used")
        rows_in = [[ph.sem(f"rows_in{b}_{k}") for k in range(TILES)] for b in range(2)]
        idx_done, unpacked, vec, turned = ph.sem("idx_done"), ph.sem("unpacked"), ph.sem("vec"), ph.sem("turned")
        packed_done = ph.sem("packed_done")
        packed_out = [ph.sem(f"packed_out{b}") for b in range(2)]
        carried = ph.sem("carried")
        scores_dram = scores.rearrange("(p j) h -> p j h", p=P)
        by_row = "(p j) -> p j"

        with nc.Block() as block:
            @block.sync
            def _(sp):
                sp.dma_start(src[:], io["src"].rearrange(by_row, p=P)).then_inc(src_in, 16)
                sp.dma_start(dst[:], io["dst"].rearrange(by_row, p=P)).then_inc(dst_in, 16)
                sp.dma_start(near[:], io["dst_before"].rearrange(by_row, p=P)).then_inc(near_in, 16)
                sp.wait_ge(near_used, 1)
                sp.dma_start(near[:], io["dst_after"].rearrange(by_row, p=P)).then_inc(near_in, 16)
                for n in range(2 * TILES):
                    sp.wait_ge(packed_done, n + 1)
                    sp.dma_start(scores_dram[:, n * chunk:(n + 1) * chunk], packed[:, n % 2])\
                        .then_inc(packed_out[n % 2], 16)
                for b in range(2):
                    sp.wait_ge(packed_out[b], 16 * TILES)

            @block.gpsimd
            def _(pool):
                def pair(i, first, last):
                    for b in range(2):
                        g = 2 * i + b
                        wait_alone(pool, idx_done, g + 1)
                        if not first:
                            wait_alone(pool, unpacked, g - 1)
                        for k in range(TILES):
                            nc.gpsimd.indirect_dma_start(rows[:, b, k], None, att,
                                                         bass.IndirectOffsetOnAxis(idx[:, b, k:k + 1], 0))\
                                .then_inc(rows_in[b][k], 16)
                in_pairs(pool, GROUPS, pair)
                for b in range(2):
                    for k in range(TILES):
                        pool.wait_ge(rows_in[b][k], 16 * GROUPS // 2)

            @block.vector
            def _(dve):
                count = [0]

                def step(ins):
                    count[0] += 1
                    ins.then_inc(vec, 1)
                    dve.wait_ge(vec, count[0])

                dve.wait_ge(dst_in, 16)
                for n, to in enumerate((starts, ends)):
                    dve.wait_ge(near_in, 16 * (n + 1))
                    nc.vector.tensor_tensor(to[:], dst[:], near[:], ALU.not_equal).then_inc(near_used, 1)
                    dve.wait_ge(near_used, n + 1)
                    step(nc.vector.tensor_scalar(to[:], to[:], NEG, None, ALU.mult))

                def indices(g, b):
                    nc.vector.tensor_copy(idx[:, b], src[:, bass.ds(g * TILES, TILES)]).then_inc(idx_done, 1)

                def pair(i, first, last):
                    if first:
                        dve.wait_ge(src_in, 16)
                        indices(0, 0)
                        indices(1, 1)
                    for b in range(2):
                        g = 2 * i + b
                        for k in range(TILES):
                            dve.wait_ge(rows_in[b][k], 16 * (i + 1))
                        nc.vector.tensor_copy(own[:, :, bass.ds(g * TILES, TILES)],
                                              rows[:, b, :, 0:HEADS].rearrange("p k h -> p h k")).then_inc(unpacked, 1)
                        if not last:
                            indices(g + 2, b)
                in_pairs(dve, GROUPS, pair)
                dve.wait_ge(unpacked, GROUPS)

                def scans(to, of, marks, initial, back):
                    d = -1 if back else 1
                    for h in range(HEADS):
                        last = nc.vector.tensor_tensor_scan(
                            to[:, h, ::d], marks[:, ::d], of[:, h, ::d],
                            NEG if initial is None else initial[:, h:h + 1], ALU.add, ALU.max)
                    step(last)

                for n, (of, marks, back) in enumerate(((own, starts, False), (best, ends, True))):
                    end = 0 if back else PER_ROW - 1
                    d = -1 if back else 1
                    scans(best, of, marks, None, back)
                    step(nc.vector.tensor_copy(tail[:], best[:, :, end]))
                    step(nc.vector.tensor_reduce(broken[:], marks[:], AX, ALU.min))
                    nc.vector.tensor_copy(broken8[:], broken[:].to_broadcast([P, HEADS])).then_inc(carried, 1)
                    dve.wait_ge(turned, 2 * n + 1)
                    nc.vector.tensor_copy(tail_t[:], psum_t[0:HEADS, 0:P])
                    step(nc.vector.tensor_copy(broken_t[:], psum_b[0:HEADS, 0:P]))
                    step(nc.vector.tensor_tensor_scan(chain[:, ::d], broken_t[:, ::d], tail_t[:, ::d], NEG,
                                                      ALU.add, ALU.max))
                    step(nc.vector.memset(carry_t[:], NEG))
                    to, fro = (slice(0, P - 1), slice(1, P)) if back else (slice(1, P), slice(0, P - 1))
                    nc.vector.tensor_copy(carry_t[:, to], chain[:, fro]).then_inc(carried, 1)
                    dve.wait_ge(turned, 2 * n + 2)
                    step(nc.vector.tensor_copy(carry[:], psum_c[:, 0:HEADS]))
                    if n == 0:
                        scans(best, of, marks, carry, back)
                    else:
                        scans(best, of, marks, carry, back)

                for n in range(2 * TILES):
                    if n >= 2:
                        dve.wait_ge(packed_out[n % 2], 16 * (n // 2))
                    part = slice(n * chunk, (n + 1) * chunk)
                    for m, of in enumerate((own, best)):
                        last = nc.vector.tensor_copy(packed[:, n % 2, :, m * HEADS:(m + 1) * HEADS],
                                                     of[:, :, part].rearrange("p h j -> p j h"))
                    last.then_inc(packed_done, 1)

            @block.tensor
            def _(pe):
                for n in range(2):
                    pe.wait_ge(carried, 2 * n + 1)
                    nc.tensor.transpose(psum_t[0:HEADS, 0:P], tail[:], c["ident"][:])
                    nc.tensor.transpose(psum_b[0:HEADS, 0:P], broken8[:], c["ident"][:]).then_inc(turned, 1)
                    pe.wait_ge(carried, 2 * n + 2)
                    nc.tensor.transpose(psum_c[:, 0:HEADS], carry_t[:], c["ident"][0:HEADS, 0:HEADS])\
                        .then_inc(turned, 1)


def attend_edges(nc, io, c, xpa, att, scores, sums):
    with Phase(nc, "att") as ph:
        ids = ph.sb("ids", [P, 2, 2 * TILES], I32)
        sc = ph.sb("sc", [P, 2, TILES, 2, HEADS])
        ai = ph.sb("ai", [WINDOW, 2, HEADS])
        xg = ph.sb("xg", [P, 2, TILES, FEAT + HEADS])
        agg_s = ph.sb("agg_s", [P, 2, FEAT + HEADS])
        rel = ph.sb("rel", [P, TILES])
        sel = ph.sb("sel", [P, 2, TILES, WINDOW])
        sel_t = ph.sb("sel_t", [WINDOW, TILES, P])
        raw = ph.sb("raw", [P, TILES, 2, HEADS])
        leaky = ph.sb("leaky", [P, TILES, 2, HEADS])
        below = ph.sb("below", [P, TILES, HEADS])
        psum_s = ph.ps("s", [WINDOW, 4, 4, P])
        psum_i = ph.ps("i", [P, 512])
        psum_a = [ph.ps(f"a{b}", [P, 512]) for b in range(2)]
        meta_in = [ph.sem(f"meta_in{b}") for b in range(2)]
        rows_in = [[ph.sem(f"rows_in{b}_{k}") for k in range(TILES)] for b in range(2)]
        rel_done, sel_done, turned = ph.sem("rel_done"), ph.sem("sel_done"), ph.sem("turned")
        turned_copied, ai_done = ph.sem("turned_copied"), ph.sem("ai_done")
        raw_done, leaky_done, below_done, prob_done = (ph.sem(n) for n in ("raw", "leaky", "below", "prob_done"))
        msg_done, agg_done = ph.sem("msg_done"), ph.sem("agg_done")
        copied, added = ph.sem("agg_copied"), ph.sem("added")
        place = place_windows(nc, c, ph, psum_a[0])

        def one_round():
            place()
            with nc.Block() as block:
                @block.sync
                def _(sp):
                    def pair(i, first, last):
                        for b in range(2):
                            g = 2 * i + b
                            if not first:
                                wait_alone(sp, msg_done, TILES * (g - 1))
                                wait_alone(sp, ai_done, g - 1)
                            sp.dma_start(ids[:, b], io["ids"][bass.ds(g, 1)].rearrange("o p k -> (o p) k"))\
                                .then_inc(meta_in[b], 16)
                            sp.dma_start(sc[:, b], scores[bass.ds(g * GROUP, GROUP), :]
                                         .rearrange("(p k) (m h) -> p k m h", p=P, m=2)).then_inc(meta_in[b], 16)
                            at = sp.value_load(c["start_i"][0:1, bass.ds(g, 1)], min_val=0, max_val=NODES_PAD)
                            sp.dma_start(ai[:, b], att[bass.ds(at, WINDOW), HEADS:2 * HEADS]).then_inc(meta_in[b], 16)
                    in_pairs(sp, GROUPS, pair)

                @block.gpsimd
                def _(pool):
                    def add_sums(g, b, first):
                        wait_alone(pool, copied, g + 1)
                        if not first:
                            wait_alone(pool, added, 16 * g)
                        at = pool.value_load(c["start_i"][0:1, bass.ds(g, 1)], min_val=0, max_val=NODES_PAD)
                        pool.dma_start(sums[bass.ds(at, WINDOW), :], agg_s[:, b], accum_op=ALU.add)\
                            .then_inc(added, 16)

                    def pair(i, first, last):
                        for b in range(2):
                            g = 2 * i + b
                            wait_alone(pool, meta_in[b], 48 * (i + 1))
                            for k in range(TILES):
                                if not first:
                                    wait_alone(pool, agg_done, TILES * (g - 2) + k + 1)
                                nc.gpsimd.indirect_dma_start(xg[:, b, k], None, xpa,
                                                             bass.IndirectOffsetOnAxis(ids[:, b, k:k + 1], 0))\
                                    .then_inc(rows_in[b][k], 16)
                                if k == ADD_AT and not first:
                                    add_sums(g - 2, b, b == 0 and is_pair(i, 1))
                        if last:
                            add_sums(GROUPS - 2, 0, False)
                            add_sums(GROUPS - 1, 1, False)
                            pool.wait_ge(added, 16 * GROUPS)
                    in_pairs(pool, GROUPS, pair, 2)
                    for b in range(2):
                        for k in range(TILES):
                            pool.wait_ge(rows_in[b][k], 16 * GROUPS // 2)

                @block.tensor
                def _(pe):
                    def turn(g, b, first):
                        wait_alone(pe, sel_done, g + 1)
                        if not first:
                            wait_alone(pe, turned_copied, g)
                        for k in range(TILES):
                            last_mm = nc.tensor.transpose(psum_s[:, k // 4, k % 4], sel[:, b, k], c["ident"][:])
                        last_mm.then_inc(turned, 1)

                    def spread(g, b, i, first):
                        pe.wait_ge(turned_copied, g + 1)
                        pe.wait_ge(meta_in[b], 48 * (i + 1))
                        if not first:
                            pe.wait_ge(raw_done, g)
                        for k in range(TILES):
                            last_mm = nc.tensor.matmul(psum_i[:, k * HEADS:(k + 1) * HEADS], sel_t[:, k], ai[:, b],
                                                       start=True, stop=True, skip_group_check=True)
                        last_mm.then_inc(ai_done, 1)

                    def pair(i, first, last):
                        if first:
                            turn(0, 0, True)
                            spread(0, 0, 0, True)
                        for b in range(2):
                            g = 2 * i + b
                            last_g = last and b == 1
                            for k in range(TILES):
                                if k == 0 and not first:
                                    pe.wait_ge(copied, g - 1)
                                pe.wait_ge(msg_done, TILES * g + k + 1)
                                nc.tensor.matmul(psum_a[b][:, 0:FEAT + HEADS], sel[:, b, k], xg[:, b, k],
                                                 start=(k == 0), stop=(k == TILES - 1)).then_inc(agg_done, 1)
                                if k == 3 and not last_g:
                                    turn(g + 1, 1 - b, False)
                                if k == 5 and not last_g:
                                    spread(g + 1, 1 - b, i + b, False)
                    in_pairs(pe, GROUPS, pair)

                @block.scalar
                def _(act):
                    def turn_out(g, first):
                        act.wait_ge(turned, g + 1)
                        if not first:
                            act.wait_ge(ai_done, g)
                        for q in range(math.ceil(TILES / 4)):
                            size = min(4, TILES - 4 * q)
                            last = nc.scalar.activation(sel_t[:, 4 * q:4 * q + size], psum_s[:, q, 0:size], ACT.Copy)
                        last.then_inc(turned_copied, 1)

                    def exponent(g, b, i, first):
                        act.wait_ge(below_done, g + 1)
                        for k in range(TILES):
                            act.wait_ge(rows_in[b][k], 16 * (i + 1))
                        if not first:
                            act.wait_ge(agg_done, TILES * (g - 1))
                        nc.scalar.activation(xg[:, b, :, FEAT:], below[:], ACT.Exp).then_inc(prob_done, 1)

                    def copy_out(g, b, first):
                        act.wait_ge(agg_done, TILES * (g + 1))
                        if not first:
                            act.wait_ge(added, 16 * (g - 1))
                        nc.scalar.activation(agg_s[:, b], psum_a[b][:, 0:FEAT + HEADS], ACT.Copy).then_inc(copied, 1)

                    def pair(i, first, last):
                        if first:
                            turn_out(0, True)
                            exponent(0, 0, 0, True)
                        for b in range(2):
                            g = 2 * i + b
                            if not (first and b == 0):
                                copy_out(g - 1, 1 - b, first or (b == 0 and is_pair(i, 1)))
                            if not (last and b == 1):
                                turn_out(g + 1, False)
                                exponent(g + 1, 1 - b, i + b, first and b == 0)
                        if last:
                            copy_out(GROUPS - 1, 1, False)
                    in_pairs(act, GROUPS, pair, 2)

                @block.vector
                def _(dve):
                    def select(g, b, i, first):
                        dve.wait_ge(meta_in[b], 48 * (i + 1))
                        nc.vector.tensor_scalar(rel[:], ids[:, b, TILES:2 * TILES], c["start_b"][:, bass.ds(g, 1)],
                                                None, ALU.subtract).then_inc(rel_done, 1)
                        dve.wait_ge(rel_done, g + 1)
                        if not first:
                            dve.wait_ge(agg_done, TILES * (g - 1))
                        nc.vector.tensor_tensor(sel[:, b], rel[:].unsqueeze(2).to_broadcast([P, TILES, WINDOW]),
                                                c["ramp"][:].unsqueeze(1).to_broadcast([P, TILES, WINDOW]),
                                                ALU.is_equal).then_inc(sel_done, 1)

                    def logits(g, b, first):
                        dve.wait_ge(ai_done, g + 1)
                        shape = [P, TILES, 2, HEADS]
                        own = psum_i[:, 0:TILES * HEADS].rearrange("p (k h) -> p k h", k=TILES)
                        nc.vector.tensor_tensor(raw[:], own.unsqueeze(2).to_broadcast(shape), sc[:, b],
                                                ALU.add).then_inc(raw_done, 1)
                        dve.wait_ge(raw_done, g + 1)
                        flat = "p k m h -> p (k m h)"
                        nc.vector.scalar_tensor_tensor(out=leaky[:].rearrange(flat), in0=raw[:].rearrange(flat),
                                                       scalar=NEG_SLOPE, in1=raw[:].rearrange(flat), op0=ALU.mult,
                                                       op1=ALU.max).then_inc(leaky_done, 1)
                        dve.wait_ge(leaky_done, g + 1)
                        if not first:
                            dve.wait_ge(prob_done, g)
                        nc.vector.tensor_tensor(below[:], leaky[:, :, 0], leaky[:, :, 1],
                                                ALU.subtract).then_inc(below_done, 1)

                    def pair(i, first, last):
                        if first:
                            select(0, 0, 0, True)
                            logits(0, 0, True)
                        for b in range(2):
                            g = 2 * i + b
                            last_g = last and b == 1
                            for k in range(TILES):
                                if k == 0:
                                    dve.wait_ge(prob_done, g + 1)
                                dve.wait_ge(rows_in[b][k], 16 * (i + 1))
                                x = xg[:, b, k, 0:FEAT].rearrange("p (h d) -> p h d", h=HEADS)
                                nc.vector.tensor_tensor(
                                    x, x, xg[:, b, k, FEAT:].unsqueeze(2).to_broadcast([P, HEADS, HEAD_DIM]),
                                    ALU.mult).then_inc(msg_done, 1)
                                if k == 2 and not last_g:
                                    select(g + 1, 1 - b, i + b, first and b == 0)
                                if k == TILES - 1 and not last_g:
                                    logits(g + 1, 1 - b, False)
                    in_pairs(dve, GROUPS, pair)
            ph.clear()
        rounds(nc, c, one_round)


def attend_in_order(nc, io, c, xpa, att, sums):
    LINE = TILES + 2
    WIDE = FEAT + HEADS
    with Phase(nc, "ord") as ph:
        ids = ph.sb("ids", [P, 2, 2 * TILES], I32)
        near = ph.sb("near", [P, 2, 2, TILES], I32)
        ai = ph.sb("ai", [WINDOW, 2, HEADS])
        xg = ph.sb("xg", [P, 2, TILES, WIDE])
        agg_s = ph.sb("agg_s", [P, 2, WIDE])
        rel = ph.sb("rel", [P, TILES])
        sel = ph.sb("sel", [P, 2, TILES, WINDOW])
        sel_t = ph.sb("sel_t", [WINDOW, TILES, P])
        row_no = ph.sb("row_no", [P, 1])
        step_f = ph.sb("step_f", [P, GROUPS])
        hand = ph.sb("hand", [P, GROUPS])
        hand_col = ph.sb("hand_col", [P, 2])
        first_row = ph.sb("first_row", [1, P])
        change = ph.sb("change", [P, 2, TILES])
        any_change = ph.sb("any_change", [P, 2])
        broken = ph.sb("broken", [P, 2, HEADS])
        marks = ph.sb("marks", [P, 2, HEADS, LINE])
        own = ph.sb("own", [P, HEADS, LINE])
        ahead = ph.sb("ahead", [P, HEADS, LINE])
        back = ph.sb("back", [P, HEADS, LINE])
        best = ph.sb("best", [P, HEADS, LINE])
        chain_f = ph.sb("chain_f", [HEADS, 2, P + 1])
        chain_b = ph.sb("chain_b", [HEADS, P + 1])
        broken_t = ph.sb("broken_t", [HEADS, 2, P])
        raw = ph.sb("raw", [P, TILES, 2, HEADS])
        leaky = ph.sb("leaky", [P, TILES, 2, HEADS])
        below = ph.sb("below", [P, TILES, HEADS])
        last_top = ph.sb("last_top", [P, 2, HEADS])
        drop = ph.sb("drop", [1, HEADS])
        shrink = ph.sb("shrink", [1, HEADS])
        carry = ph.sb("carry", [1, WIDE])
        psum_s = ph.ps("s", [WINDOW, 4, 4, P])
        psum_i = ph.ps("i", [P, 512])
        psum_m = ph.ps("m", [P, 4, P])
        psum_a = [ph.ps(f"a{b}", [P, 512]) for b in range(2)]
        meta_in = [ph.sem(f"meta_in{b}") for b in range(2)]
        rows_in = [[ph.sem(f"rows_in{b}_{k}") for k in range(TILES)] for b in range(2)]
        numbered, stepped, set_up = ph.sem("numbered"), ph.sem("stepped"), ph.sem("set_up")
        rel_done, sel_done, turned = ph.sem("rel_done"), ph.sem("sel_done"), ph.sem("turned")
        turned_copied, ai_done = ph.sem("turned_copied"), ph.sem("ai_done")
        changes, broke, prepared = ph.sem("changes"), ph.sem("broke"), ph.sem("prepared")
        own_done, ends_done, ends_turned = ph.sem("own_done"), ph.sem("ends_done"), ph.sem("ends_turned")
        started, chained, carries = ph.sem("started"), ph.sem("chained"), ph.sem("carries")
        best_done, ahead_done, own_carried = ph.sem("best_done"), ph.sem("ahead_done"), ph.sem("own_carried")
        raw_done, leaky_done, below_done, prob_done = (ph.sem(n) for n in ("raw", "leaky", "below", "prob_done"))
        top_done, handed, drop_part, drop_done = (ph.sem(n) for n in ("top_done", "handed", "drop_part", "drop_done"))
        shrunk, carry_done = ph.sem("shrunk"), ph.sem("carry_done")
        msg_done, agg_done, summed = ph.sem("msg_done"), ph.sem("agg_done"), ph.sem("summed")
        copied, stored = ph.sem("agg_copied"), ph.sem("stored")
        line = "p h k -> p (h k)"
        handed_rows = psum_m[0:1].rearrange("o q f -> o (q f)")
        spread_carries = psum_m[:].rearrange("p q f -> p (q f)")

        place_windows(nc, c, ph, psum_a[0])()
        with nc.Block() as block:
            @block.gpsimd
            def _(pool):
                nc.gpsimd.iota(row_no[:], [[0, 1]], base=0, channel_multiplier=1,
                               allow_small_or_imprecise_dtypes=True).then_inc(numbered, 1)

            @block.vector
            def _(dve):
                nc.vector.memset(hand[:], 0.0)
                nc.vector.memset(marks[:], NEG)
                nc.vector.memset(own[:], NEG)
                nc.vector.memset(chain_b[:], NEG)
                nc.vector.memset(chain_f[:], NEG)
                nc.vector.tensor_copy(first_row[:], c["ident"][0:1, :]).then_inc(set_up, 1)
                nc.vector.tensor_tensor(step_f[:, 1:], c["start_b"][:, 1:], c["start_b"][:, 0:GROUPS - 1],
                                        ALU.subtract).then_inc(stepped, 1)
                dve.wait_ge(stepped, 1)
                dve.wait_ge(set_up, 1)
                dve.wait_ge(numbered, 1)
                nc.vector.tensor_scalar(hand[:, 1:], step_f[:, 1:], row_no[:], None, ALU.is_equal)\
                    .then_inc(set_up, 1)

        with nc.Block() as block:
            @block.sync
            def _(sp):
                def store(g, b, first):
                    wait_alone(sp, copied, g + 1)
                    if not first:
                        wait_alone(sp, stored, 16 * g)
                    at = sp.value_load(c["start_i"][0:1, bass.ds(g, 1)], min_val=0, max_val=NODES_PAD)
                    sp.dma_start(sums[bass.ds(at, WINDOW), :], agg_s[:, b]).then_inc(stored, 16)

                def pair(i, first, last):
                    for b in range(2):
                        g = 2 * i + b
                        if not first:
                            wait_alone(sp, msg_done, TILES * (g - 1))
                            wait_alone(sp, ai_done, g - 1)
                        sp.dma_start(ids[:, b], io["ids"][bass.ds(g, 1)].rearrange("o p k -> (o p) k"))\
                            .then_inc(meta_in[b], 16)
                        sp.dma_start(near[:, b].rearrange("p d k -> p (d k)"),
                                     io["near"][bass.ds(g, 1)].rearrange("o p k -> (o p) k")).then_inc(meta_in[b], 16)
                        at = sp.value_load(c["start_i"][0:1, bass.ds(g, 1)], min_val=0, max_val=NODES_PAD)
                        sp.dma_start(ai[:, b], att[bass.ds(at, WINDOW), HEADS:2 * HEADS]).then_inc(meta_in[b], 16)
                        if not first:
                            store(g - 2, b, b == 0 and is_pair(i, 1))
                    if last:
                        store(GROUPS - 2, 0, False)
                        store(GROUPS - 1, 1, False)
                        sp.wait_ge(stored, 16 * GROUPS)
                in_pairs(sp, GROUPS, pair, 2)

            @block.gpsimd
            def _(pool):
                def pair(i, first, last):
                    for b in range(2):
                        g = 2 * i + b
                        wait_alone(pool, meta_in[b], 48 * (i + 1))
                        for k in range(TILES):
                            if not first:
                                wait_alone(pool, agg_done, TILES * (g - 2) + k + 1)
                            nc.gpsimd.indirect_dma_start(xg[:, b, k], None, xpa,
                                                         bass.IndirectOffsetOnAxis(ids[:, b, k:k + 1], 0))\
                                .then_inc(rows_in[b][k], 16)
                in_pairs(pool, GROUPS, pair)
                for b in range(2):
                    for k in range(TILES):
                        pool.wait_ge(rows_in[b][k], 16 * GROUPS // 2)

            @block.tensor
            def _(pe):
                def turn(g, b, first):
                    wait_alone(pe, sel_done, g + 1)
                    if not first:
                        wait_alone(pe, turned_copied, g)
                    for k in range(TILES):
                        last_mm = nc.tensor.transpose(psum_s[:, k // 4, k % 4], sel[:, b, k], c["ident"][:])
                    last_mm.then_inc(turned, 1)

                def spread(g, b, i, first):
                    pe.wait_ge(turned_copied, g + 1)
                    pe.wait_ge(meta_in[b], 48 * (i + 1))
                    if not first:
                        pe.wait_ge(raw_done, g)
                    for k in range(TILES):
                        last_mm = nc.tensor.matmul(psum_i[:, k * HEADS:(k + 1) * HEADS], sel_t[:, k], ai[:, b],
                                                   start=True, stop=True, skip_group_check=True)
                    last_mm.then_inc(ai_done, 1)

                def carry_maxima(g, first, second):
                    wait_alone(pe, prepared, g + 1)
                    wait_alone(pe, ends_done, g + 1)
                    if not first and not second:
                        wait_alone(pe, carry_done, g - 1)
                    for d, of in enumerate((ahead[:, :, TILES], back[:, :, 1])):
                        nc.tensor.transpose(psum_m[0:HEADS, 2 * d], of, c["ident"][:])
                        last_mm = nc.tensor.transpose(psum_m[0:HEADS, 2 * d + 1], broken[:, d], c["ident"][:])
                    last_mm.then_inc(ends_turned, 1)
                    wait_alone(pe, chained, g + 1)
                    for d, of in enumerate((chain_f[:, g_buffer[0], 0:P], chain_b[:, 1:P + 1])):
                        last_mm = nc.tensor.transpose(spread_carries[:, d * HEADS:(d + 1) * HEADS], of,
                                                      c["ident"][0:HEADS, 0:HEADS])
                    last_mm.then_inc(carries, 1)

                g_buffer = [0]

                def hand_on(g, b):
                    pe.wait_ge(best_done, g + 1)
                    pe.wait_ge(copied, g)
                    pe.wait_ge(top_done, g)
                    nc.tensor.matmul(handed_rows[:, 0:WIDE], hand_col[:, b:b + 1], agg_s[:, 1 - b],
                                     start=True, stop=True, skip_group_check=True)
                    nc.tensor.matmul(handed_rows[:, WIDE:WIDE + HEADS], c["ident"][:, P - 1:P], last_top[:, 1 - b],
                                     start=True, stop=True, skip_group_check=True).then_inc(handed, 1)

                def pair(i, first, last):
                    if first:
                        turn(0, 0, True)
                        spread(0, 0, 0, True)
                    for b in range(2):
                        g = 2 * i + b
                        last_g = last and b == 1
                        g_buffer[0] = b
                        carry_maxima(g, first and b == 0, first and b == 1)
                        if not (first and b == 0):
                            hand_on(g, b)
                        for k in range(TILES):
                            if k == 0 and not first:
                                pe.wait_ge(copied, g - 1)
                            pe.wait_ge(msg_done, TILES * g + k + 1)
                            nc.tensor.matmul(psum_a[b][:, 0:WIDE], sel[:, b, k], xg[:, b, k], start=(k == 0),
                                             stop=(k == TILES - 1 and first and b == 0),
                                             skip_group_check=True).then_inc(agg_done, 1)
                            if k == 3 and not last_g:
                                turn(g + 1, 1 - b, False)
                            if k == 8 and not last_g:
                                spread(g + 1, 1 - b, i + b, False)
                        if first and b == 0:
                            pe.wait_ge(agg_done, TILES)
                            pe.nop().then_inc(summed, 1)
                        else:
                            pe.wait_ge(carry_done, g)
                            nc.tensor.matmul(psum_a[b][:, 0:WIDE], first_row[:], carry[:], start=False, stop=True,
                                             skip_group_check=True).then_inc(summed, 1)
                in_pairs(pe, GROUPS, pair)

            @block.scalar
            def _(act):
                def turn_out(g, first):
                    act.wait_ge(turned, g + 1)
                    if not first:
                        act.wait_ge(ai_done, g)
                    for q in range(math.ceil(TILES / 4)):
                        size = min(4, TILES - 4 * q)
                        last = nc.scalar.activation(sel_t[:, 4 * q:4 * q + size], psum_s[:, q, 0:size], ACT.Copy)
                    last.then_inc(turned_copied, 1)

                def copy_out(g, b, free):
                    act.wait_ge(summed, g + 1)
                    if not free:
                        act.wait_ge(stored, 16 * (g - 1))
                    nc.scalar.activation(agg_s[:, b], psum_a[b][:, 0:WIDE], ACT.Copy).then_inc(copied, 1)

                def pair(i, first, last):
                    if first:
                        turn_out(0, True)
                    for b in range(2):
                        g = 2 * i + b
                        act.wait_ge(below_done, g + 1)
                        nc.scalar.activation(xg[:, b, :, FEAT:], below[:], ACT.Exp).then_inc(prob_done, 1)
                        if not (first and b == 0):
                            act.wait_ge(drop_done, g)
                            nc.scalar.activation(shrink[:], drop[:], ACT.Exp).then_inc(shrunk, 1)
                        if not (last and b == 1):
                            turn_out(g + 1, False)
                        copy_out(g, b, first)
                in_pairs(act, GROUPS, pair)

            @block.vector
            def _(dve):
                def prepare(g, b, i, first):
                    dve.wait_ge(meta_in[b], 48 * (i + 1))
                    nc.vector.tensor_scalar(rel[:], ids[:, b, TILES:2 * TILES], c["start_b"][:, bass.ds(g, 1)],
                                            None, ALU.subtract).then_inc(rel_done, 1)
                    nc.vector.tensor_tensor(
                        change[:], ids[:, b, TILES:2 * TILES].unsqueeze(1).to_broadcast([P, 2, TILES]), near[:, b],
                        ALU.not_equal).then_inc(changes, 1)
                    dve.wait_ge(rel_done, g + 1)
                    if not first:
                        dve.wait_ge(agg_done, TILES * (g - 1))
                    nc.vector.tensor_tensor(sel[:, b], rel[:].unsqueeze(2).to_broadcast([P, TILES, WINDOW]),
                                            c["ramp"][:].unsqueeze(1).to_broadcast([P, TILES, WINDOW]),
                                            ALU.is_equal).then_inc(sel_done, 1)
                    dve.wait_ge(changes, g + 1)
                    nc.vector.tensor_reduce(any_change[:], change[:], AX, ALU.max).then_inc(broke, 1)
                    for d in range(2):
                        nc.vector.tensor_scalar(marks[:, d, :, 1:TILES + 1],
                                                change[:, d:d + 1].to_broadcast([P, HEADS, TILES]), NEG, None,
                                                ALU.mult)
                    nc.vector.tensor_copy(hand_col[:, b:b + 1], hand[:, bass.ds(g, 1)])
                    dve.wait_ge(broke, g + 1)
                    nc.vector.tensor_scalar(broken[:], any_change[:].unsqueeze(2).to_broadcast([P, 2, HEADS]), NEG,
                                            None, ALU.mult).then_inc(prepared, 1)

                def scan(to, of, d, initial=NEG):
                    step = -1 if d else 1
                    return nc.vector.tensor_tensor_scan(
                        to[:].rearrange(line)[:, ::step], marks[:, d].rearrange(line)[:, ::step],
                        of[:].rearrange(line)[:, ::step], initial, ALU.add, ALU.max)

                def maxima(g, b, i, first):
                    for k in range(TILES):
                        dve.wait_ge(rows_in[b][k], 16 * (i + 1))
                    nc.vector.memset(own[:, :, ::LINE - 1], NEG)
                    nc.vector.tensor_copy(own[:, :, 1:TILES + 1],
                                          xg[:, b, :, FEAT:].rearrange("p k h -> p h k")).then_inc(own_done, 1)
                    dve.wait_ge(own_done, g + 1)
                    dve.wait_ge(prepared, g + 1)
                    scan(ahead, own, 0)
                    scan(back, own, 1).then_inc(ends_done, 1)
                    if first:
                        nc.vector.memset(chain_f[:, b, 0:1], NEG).then_inc(started, 1)
                    else:
                        nc.vector.tensor_copy(chain_f[:, b, 0:1], chain_f[:, 1 - b, P:P + 1]).then_inc(started, 1)
                    dve.wait_ge(ends_turned, g + 1)
                    nc.vector.tensor_copy(broken_t[:], psum_m[0:HEADS, 1::2]).then_inc(started, 1)
                    dve.wait_ge(started, 2 * g + 2)
                    nc.vector.tensor_tensor_scan(chain_f[:, b, 1:P + 1], broken_t[:, 0], psum_m[0:HEADS, 0],
                                                 chain_f[:, b, 0:1], ALU.add, ALU.max)
                    nc.vector.tensor_tensor_scan(chain_b[:, P - 1::-1], broken_t[:, 1, ::-1],
                                                 psum_m[0:HEADS, 2, ::-1], NEG, ALU.add,
                                                 ALU.max).then_inc(chained, 1)
                    dve.wait_ge(carries, g + 1)
                    nc.vector.tensor_copy(own[:, :, 0], spread_carries[:, 0:HEADS]).then_inc(own_carried, 1)
                    dve.wait_ge(own_carried, g + 1)
                    scan(ahead, own, 0).then_inc(ahead_done, 1)
                    dve.wait_ge(ahead_done, 2 * g + 1)
                    nc.vector.tensor_copy(ahead[:, :, LINE - 1], spread_carries[:, HEADS:2 * HEADS])\
                        .then_inc(ahead_done, 1)
                    dve.wait_ge(ahead_done, 2 * g + 2)
                    scan(best, ahead, 1).then_inc(best_done, 1)

                def logits(g, b, first):
                    dve.wait_ge(ai_done, g + 1)
                    dve.wait_ge(best_done, g + 1)
                    mine = psum_i[:, 0:TILES * HEADS].rearrange("p (k h) -> p k h", k=TILES)
                    nc.vector.tensor_tensor(raw[:, :, 0], mine, xg[:, b, :, FEAT:], ALU.add)
                    nc.vector.tensor_tensor(raw[:, :, 1], mine,
                                            best[:, :, 1:TILES + 1].rearrange("p h k -> p k h"),
                                            ALU.add).then_inc(raw_done, 1)
                    dve.wait_ge(raw_done, g + 1)
                    flat = "p k m h -> p (k m h)"
                    nc.vector.scalar_tensor_tensor(out=leaky[:].rearrange(flat), in0=raw[:].rearrange(flat),
                                                   scalar=NEG_SLOPE, in1=raw[:].rearrange(flat), op0=ALU.mult,
                                                   op1=ALU.max).then_inc(leaky_done, 1)
                    dve.wait_ge(leaky_done, g + 1)
                    if not first:
                        dve.wait_ge(prob_done, g)
                    nc.vector.tensor_tensor(below[:], leaky[:, :, 0], leaky[:, :, 1],
                                            ALU.subtract).then_inc(below_done, 1)
                    nc.vector.tensor_copy(last_top[:, b], leaky[:, TILES - 1, 1]).then_inc(top_done, 1)
                    if not first:
                        dve.wait_ge(handed, g)
                        nc.vector.tensor_tensor(drop[:], handed_rows[:, WIDE:WIDE + HEADS], leaky[0:1, 0, 1],
                                                ALU.subtract).then_inc(drop_part, 1)
                        dve.wait_ge(drop_part, g)
                        nc.vector.tensor_scalar(drop[:], drop[:], 0.0, None, ALU.min).then_inc(drop_done, 1)

                def scale_carry(g):
                    dve.wait_ge(shrunk, g)
                    nc.vector.tensor_tensor(
                        carry[:, 0:FEAT].rearrange("o (h d) -> o h d", h=HEADS),
                        handed_rows[:, 0:FEAT].rearrange("o (h d) -> o h d", h=HEADS),
                        shrink[:].unsqueeze(2).to_broadcast([1, HEADS, HEAD_DIM]), ALU.mult)
                    nc.vector.tensor_tensor(carry[:, FEAT:], handed_rows[:, FEAT:WIDE], shrink[:],
                                            ALU.mult).then_inc(carry_done, 1)

                def pair(i, first, last):
                    if first:
                        prepare(0, 0, 0, True)
                    for b in range(2):
                        g = 2 * i + b
                        first_g = first and b == 0
                        maxima(g, b, i, first_g)
                        logits(g, b, first_g)
                        for k in range(TILES):
                            if k == 0:
                                dve.wait_ge(prob_done, g + 1)
                            x = xg[:, b, k, 0:FEAT].rearrange("p (h d) -> p h d", h=HEADS)
                            nc.vector.tensor_tensor(
                                x, x, xg[:, b, k, FEAT:].unsqueeze(2).to_broadcast([P, HEADS, HEAD_DIM]),
                                ALU.mult).then_inc(msg_done, 1)
                            if k == 2 and not (last and b == 1):
                                prepare(g + 1, 1 - b, i + b, first_g)
                            if k == 5 and not first_g:
                                scale_carry(g)
                in_pairs(dve, GROUPS, pair)


def end_attention(nc, io, c, heads, x1, out_dram):
    with Phase(nc, "end") as ph:
        ln_row = ph.sb("ln_row", [1, 2 * FEAT])
        ones = ph.sb("ones", [1, P])
        ln_wb = ph.sb("ln_wb", [P, 2, FEAT])
        shape = [P, 2, BATCH, FEAT]
        rows = ph.sb("rows", [P, 2, BATCH, FEAT + HEADS])
        xn = ph.sb("xn", shape)
        inv = ph.sb("inv", [P, 2, BATCH, HEADS])
        o = ph.sb("o", [P, BATCH, FEAT])
        u = ph.sb("u", shape)
        low = ph.sb("low", shape)
        pre = ph.sb("pre", [P, BATCH, FEAT])
        res = ph.sb("res", shape)
        stats = ph.sb("stats", [P, 2, BATCH, 6])
        mean_var = ph.sb("mean_var", [P, 2, BATCH, 2])
        std = ph.sb("std", [P, 2, BATCH])
        rstd = ph.sb("rstd", [P, 2, BATCH])
        bias = ph.sb("bias", [P, 2, BATCH])
        psum_ln = ph.ps("ln", [P, 512])
        ln_in, one_set, ln_spread, ln_made = ph.sem("ln_in"), ph.sem("one_set"), ph.sem("ln_spread"), ph.sem("ln_made")
        rows_in = [ph.sem(f"rows_in{b}") for b in range(2)]
        x_in = [ph.sem(f"x_in{b}") for b in range(2)]
        stored = [ph.sem(f"stored{b}") for b in range(2)]
        sum_done, inv_done, o_done = ph.sem("sum_done"), ph.sem("inv_done"), ph.sem("o_done")
        stat_done, var_done, std_done = ph.sem("stat_done"), ph.sem("var_done"), ph.sem("std_done")
        rstd_done, bias_done, normed = ph.sem("rstd_done"), ph.sem("bias_done"), ph.sem("normed")
        weighed, u_done, low_done, exp_done = (ph.sem(n) for n in ("weighed", "u_done", "low_done", "exp_done"))
        elu_done, pre_done, out_done = ph.sem("elu_done"), ph.sem("pre_done"), ph.sem("out_done")
        flat = "p j f -> p (j f)"

        with nc.Block() as block:
            @block.sync
            def _(sp):
                sp.dma_start(ln_row[:, 0:FEAT], io["ln_w"].rearrange("(o f) -> o f", o=1)).then_inc(ln_in, 16)
                sp.dma_start(ln_row[:, FEAT:], io["ln_b"].rearrange("(o f) -> o f", o=1)).then_inc(ln_in, 16)

                def load(s, b):
                    sp.dma_start(rows[:, b].rearrange(flat), batch_rows(heads, s)).then_inc(rows_in[b], 16)
                    sp.dma_start(xn[:, b].rearrange(flat), batch_rows(x1, s)).then_inc(x_in[b], 16)

                def store(s, b):
                    wait_alone(sp, out_done, s + 1)
                    sp.dma_start(batch_rows(out_dram, s), res[:, b].rearrange(flat)).then_inc(stored[b], 16)

                def pair(i, first, last):
                    if first:
                        load(0, 0)
                        load(1, 1)
                    for b in range(2):
                        s = 2 * i + b
                        store(s, b)
                        if not last:
                            load(s + 2, b)
                in_pairs(sp, BATCHES, pair)
                for b in range(2):
                    sp.wait_ge(stored[b], 16 * BATCHES // 2)

            @block.tensor
            def _(pe):
                pe.wait_ge(ln_in, 32)
                pe.wait_ge(one_set, 1)
                nc.tensor.matmul(psum_ln[:], ones[:], ln_row[:], start=True, stop=True).then_inc(ln_spread, 1)

            @block.gpsimd
            def _(pool):
                def pair(i, first, last):
                    for b in range(2):
                        s = 2 * i + b
                        wait_alone(pool, u_done, s + 1)
                        if not first:
                            wait_alone(pool, elu_done, s - 1)
                        nc.gpsimd.tensor_scalar(low[:, b], u[:, b], 0.0, None, ALU.min).then_inc(low_done, 1)
                in_pairs(pool, BATCHES, pair)

            @block.scalar
            def _(act):
                def root(s, b, n):
                    act.wait_ge(var_done, BATCH * (2 * s + n + 1) if n == 0 else BATCH * (2 * s + 2))
                    nc.scalar.activation(std[:, n], mean_var[:, n, :, 1], ACT.Sqrt, bias=c["ln_eps"][:])\
                        .then_inc(std_done, 1)

                def norm(to, of, n, sem):
                    for j in range(BATCH):
                        nc.scalar.activation(to[:, j], of[:, j], ACT.Identity, scale=rstd[:, n, j:j + 1],
                                             bias=bias[:, n, j:j + 1]).then_inc(sem, 1)

                def pair(i, first, last):
                    for b in range(2):
                        s = 2 * i + b
                        root(s, b, 0)
                        act.wait_ge(bias_done, 2 * s + 1)
                        norm(u[:, b], o, 0, normed)
                        act.wait_ge(low_done, s + 1)
                        nc.scalar.activation(low[:, b], low[:, b], ACT.Exp).then_inc(exp_done, 1)
                        root(s, b, 1)
                        act.wait_ge(bias_done, 2 * s + 2)
                        if not first:
                            act.wait_ge(stored[b], 16 * i)
                        for j in range(BATCH):
                            a = nc.scalar.activation(res[:, b, j], pre[:, j], ACT.Identity,
                                                     scale=rstd[:, 1, j:j + 1], bias=bias[:, 1, j:j + 1])
                        a.then_inc(out_done, 1)
                in_pairs(act, BATCHES, pair)

            @block.vector
            def _(dve):
                nc.vector.memset(ones[:], 1.0).then_inc(one_set, 1)
                dve.wait_ge(ln_spread, 1)
                nc.vector.tensor_copy(ln_wb[:].rearrange("p a f -> p (a f)"), psum_ln[:]).then_inc(ln_made, 1)
                dve.wait_ge(ln_made, 1)

                def norms(x, n, count):
                    for j in range(BATCH):
                        nc.vector.bn_stats(stats[:, n, j], x[:, j]).then_inc(stat_done, 1)
                    wait_alone(dve, stat_done, BATCH * count)
                    for j in range(BATCH):
                        nc.vector.bn_aggr(mean_var[:, n, j], stats[:, n, j]).then_inc(var_done, 1)
                    dve.wait_ge(std_done, count)
                    nc.vector.reciprocal(rstd[:, n], std[:, n]).then_inc(rstd_done, 1)
                    dve.wait_ge(rstd_done, count)
                    nc.vector.scalar_tensor_tensor(out=bias[:, n], in0=mean_var[:, n, :, 0], scalar=-1.0,
                                                   in1=rstd[:, n], op0=ALU.mult, op1=ALU.mult).then_inc(bias_done, 1)

                def pair(i, first, last):
                    for b in range(2):
                        s = 2 * i + b
                        dve.wait_ge(rows_in[b], 16 * (i + 1))
                        nc.vector.tensor_scalar(inv[:, 0], rows[:, b, :, FEAT:], SOFTMAX_EPS, None,
                                                ALU.add).then_inc(sum_done, 1)
                        dve.wait_ge(sum_done, s + 1)
                        nc.vector.reciprocal(inv[:, 1], inv[:, 0]).then_inc(inv_done, 1)
                        dve.wait_ge(inv_done, s + 1)
                        for j in range(BATCH):
                            a = nc.vector.tensor_tensor(
                                o[:, j].rearrange("p (h d) -> p h d", h=HEADS),
                                rows[:, b, j, 0:FEAT].rearrange("p (h d) -> p h d", h=HEADS),
                                inv[:, 1, j].unsqueeze(2).to_broadcast([P, HEADS, HEAD_DIM]), ALU.mult)
                        a.then_inc(o_done, 1)
                        dve.wait_ge(o_done, s + 1)
                        norms(o, 0, 2 * s + 1)
                        dve.wait_ge(normed, BATCH * (s + 1))
                        wide = [P, BATCH, FEAT]
                        nc.vector.tensor_tensor(u[:, b], u[:, b], ln_wb[:, 0:1].to_broadcast(wide),
                                                ALU.mult).then_inc(weighed, 1)
                        dve.wait_ge(weighed, s + 1)
                        nc.vector.tensor_tensor(u[:, b], u[:, b], ln_wb[:, 1:2].to_broadcast(wide),
                                                ALU.add).then_inc(u_done, 1)
                        dve.wait_ge(exp_done, s + 1)
                        nc.vector.scalar_tensor_tensor(out=u[:, b].rearrange(flat), in0=u[:, b].rearrange(flat),
                                                       scalar=0.0, in1=low[:, b].rearrange(flat), op0=ALU.max,
                                                       op1=ALU.add).then_inc(elu_done, 1)
                        dve.wait_ge(elu_done, s + 1)
                        dve.wait_ge(x_in[b], 16 * (i + 1))
                        nc.vector.tensor_scalar(u[:, b], u[:, b], -1.0, None, ALU.add).then_inc(ln_made, 1)
                        dve.wait_ge(ln_made, s + 2)
                        if not (first and b == 0):
                            dve.wait_ge(out_done, s)
                        nc.vector.scalar_tensor_tensor(out=pre[:].rearrange(flat), in0=xn[:, b].rearrange(flat),
                                                       scalar=2.0, in1=u[:, b].rearrange(flat), op0=ALU.mult,
                                                       op1=ALU.add).then_inc(pre_done, 1)
                        dve.wait_ge(pre_done, s + 1)
                        norms(pre, 1, 2 * s + 2)
                in_pairs(dve, BATCHES, pair)


def gnn(nc, io, out):
    def scratch(name, shape):
        return nc.dram_tensor(name, shape, F32, kind="Internal").ap()

    y = scratch("y_rows", [NODES_PAD, FEAT])
    sums = scratch("sum_rows", [TABLE, 8 * MUL])
    heads = scratch("head_rows", [TABLE, FEAT + HEADS])
    x1 = scratch("x1_rows", [NODES_PAD, FEAT])
    xpa = scratch("xpa_rows", [NODES_PAD, FEAT + HEADS])
    att = scratch("att_rows", [TABLE, 2 * HEADS])
    scores = scratch("score_rows", [EDGES_PAD, 2 * HEADS])

    with ExitStack() as ctx:
        def keep(name, shape, dt=F32):
            return ctx.enter_context(nc.sbuf_tensor(name, shape, dt))

        c = {
            "ident": keep("ident", [P, P]), "ramp": keep("ramp", [P, WINDOW]), "one_row": keep("one_row", [1, P]),
            "ln_eps": keep("ln_eps_col", [P, 1]),
            "factor": keep("factor", [P, NODE_TILES]), "factor8": keep("factor8", [P, NODE_TILES]),
            "first_dst": keep("first_dst", [1, GROUPS], I32), "last_dst": keep("last_dst", [1, GROUPS], I32),
            "reach": keep("reach", [1, GROUPS]), "span_f": keep("span_f", [1, 1]), "span": keep("span", [1, 1], I32),
            "shift": keep("shift", [1, GROUPS]), "start_f": keep("start_f", [1, GROUPS]),
            "start_i": keep("start_i", [1, GROUPS], I32), "start_b": keep("start_b", [P, GROUPS]),
        }
        constants(nc, io, c)
        project_sources(nc, io, c, y, [sums, heads])
        start_windows(nc, c, "start0")
        convolve_edges(nc, io, c, y, sums)
        end_convolution(nc, io, c, sums, x1, xpa, att)
        start_windows(nc, c, "start1")
        span = nc.values_load(c["span"][0:1, 0:1], min_val=0, max_val=NODES_PAD)
        with nc.If(span < WINDOW):
            nc.all_engine_barrier()
            attend_in_order(nc, io, c, xpa, att, heads)
        with nc.Else():
            nc.all_engine_barrier()
            source_maxima(nc, io, c, att, scores)
            attend_edges(nc, io, c, xpa, att, scores, heads)
        end_attention(nc, io, c, heads, x1, out)


def laid_out(inputs):
    import numpy as np

    a = {k: np.ascontiguousarray(v) for k, v in inputs.items()}
    x = np.zeros((NODES_PAD, FEAT), np.float32)
    x[:NODES] = a["x"]
    order = np.concatenate([np.arange(MUL)] + [MUL + c + 3 * np.arange(MUL) for c in range(3)])
    factor = np.zeros((NODES_PAD,), np.float32)
    factor[:NODES] = a["node_vec1"][:, 0]

    def edges(v, fill, front=0):
        out = np.full((EDGES_PAD, *v.shape[1:]), fill, v.dtype)
        out[front:front + EDGES] = v
        return out

    src, dst = edges(a["src"], 0), edges(a["dst"], NODES)
    dst_before = np.concatenate([np.full(1, -1, dst.dtype), dst[:-1]])
    dst_after = np.concatenate([dst[1:], np.full(1, -1, dst.dtype)])
    grouped = (GROUPS, P, TILES)
    scalars = edges(a["edge_attr_8"], 0).reshape(GROUPS, P, 2, HALF, SCALARS).transpose(2, 4, 0, 3, 1)
    return {
        "x": x, "x_t": np.ascontiguousarray(x[:, order].reshape(BATCHES, P, BATCH, FEAT).transpose(3, 0, 2, 1))
        .reshape(FEAT, NODES_PAD),
        "node_factor": np.ascontiguousarray(factor.reshape(BATCHES, P, BATCH).transpose(1, 0, 2))
        .reshape(P, NODE_TILES),
        "src": src, "dst": dst, "dst_before": dst_before, "dst_after": dst_after,
        "ids": np.ascontiguousarray(np.concatenate([src.reshape(grouped), dst.reshape(grouped)], axis=2)),
        "near": np.ascontiguousarray(np.concatenate([dst_before.reshape(grouped), dst_after.reshape(grouped)], axis=2)),
        "edge_attr": np.ascontiguousarray(edges(a["edge_attr_4"], 0).reshape(GROUPS, P, TILES * 4)),
        "edge_scalars_t": np.ascontiguousarray(scalars).reshape(2 * SCALARS, EDGES_PAD // 2),
        "sc_w0": a["L0_gnn_sc_w0"], "sc_w1": a["L0_gnn_sc_w1"],
        "lin1_w0": a["L0_gnn_lin1_w0"], "lin1_w1": a["L0_gnn_lin1_w1"],
        "fc_w1": a["L0_gnn_fc_w1"],
        "fc_w2": a["L0_gnn_fc_w2"],
        **{f"lin2_w{n}": a[f"L0_gnn_lin2_w{n}"] for n in ("00", "01", "10", "11")},
        "lin_w": a["L1_gnn_lin_w"], "lin_w_t": np.ascontiguousarray(a["L1_gnn_lin_w"].T),
        "att_t": np.ascontiguousarray(a["L1_gnn_att"].T),
        "ln_w": a["L1_gnn_ln_w"], "ln_b": a["L1_gnn_ln_b"],
    }


def kernel(**inputs):
    import concourse.bacc as bacc
    from concourse.bass_utils import run_bass_kernel_spmd

    nc = bacc.Bacc("TRN2", target_bir_lowering=False, num_devices=1)
    arrays = {f"in_{k}_dram": v for k, v in laid_out(inputs).items()}
    io = {name[3:-5]: nc.dram_tensor(name, v.shape, mybir.dt.from_np(v.dtype), kind="ExternalInput").ap()
          for name, v in arrays.items()}
    out = nc.dram_tensor("out_0_dram", (NODES_PAD, FEAT), F32, kind="ExternalOutput").ap()
    gnn(nc, io, out)
    r = run_bass_kernel_spmd(nc, [arrays], core_ids=[0])
    return r.results[0]["out_0_dram"][:NODES]
```
